# Optimizing a Trainium2 kernel written in Bass

```python
import numpy as np
import jax
import jax.numpy as jnp

def _softmax(x, axis=-1):
    return jax.nn.softmax(x, axis=axis)

def _gelu(x):
    return jax.nn.gelu(x, approximate=True)

def _silu(x):
    return jax.nn.silu(x)

def _sigmoid(x):
    return jax.nn.sigmoid(x)

def _layernorm(x, axis=-1, eps=1e-05):
    m = jnp.mean(x, axis=axis, keepdims=True)
    v = jnp.var(x, axis=axis, keepdims=True)
    return (x - m) / jnp.sqrt(v + eps)

def _scatter_add(tgt, idx, src, axis=0):
    return tgt.at[idx].add(src)

def _segment_sum(src, seg, n):
    return jax.ops.segment_sum(src, seg, n)
kernel_name = 'mk_adj_preln_d2_adj_r2_79a6ce'

def setup_inputs(seed: int=0):
    np.random.seed(seed)
    _w = jnp.asarray

    def _rec_inputs():
        import jax
        import jax.numpy as jnp
        _gk = jax.random.key(seed)
        x = -0.000929 + 1 * jax.random.normal(jax.random.fold_in(_gk, 1), (4096, 128), jnp.float32)
        _w = (1.0 + jnp.arange(4096, dtype=jnp.float32)) ** (-0.5)
        _w = _w / _w.mean()
        _pij = jnp.clip(0.000488281 * _w[:, None] * _w[None, :], 0.0, 1.0)
        _a = jax.random.uniform(jax.random.fold_in(_gk, 2), (4096, 4096)) < _pij
        _af = _a.astype(jnp.float32)
        adj = _af
        return (x, adj)
    x, adj = _rec_inputs()

    def _L0_gnn_setup():
        import jax, jax.numpy as jnp
        import numpy as np
        N_BLOCKS = 16
        BLOCK = 256
        N = N_BLOCKS * BLOCK
        E = 128
        LAYER_NUM = 2
        NEG = -9000000000000000.0

        def _build_adj():
            filter_num = [BLOCK] * N_BLOCKS
            adj = np.zeros((N, N), dtype=np.float32)
            row = last = filter_num[0]
            for num in filter_num:
                adj[row:row + num, row - last:row] = 1.0
                row += num
                last = num
            np.fill_diagonal(adj, 0.0)
            return adj

        def _gat_layer(h, adj, W, b):
            n, e = h.shape
            att = jnp.matmul(h, h.T) / jnp.sqrt(jnp.asarray(e, h.dtype))
            A = jnp.where(adj > 0, att, jnp.asarray(NEG, h.dtype))
            A = jax.nn.softmax(A, axis=1)
            d = jnp.arange(n)
            A = A * 0.5
            A = A.at[d, d].add(0.5)
            nf1 = jnp.sum(adj[:, 0] != 0)
            mask = d < nf1
            A = jnp.where(mask[:, None], 0.0, A)
            A = A.at[d, d].set(jnp.where(mask, 1.0, A[d, d]))
            h_new = jnp.matmul(h, W.T) + b
            return jax.nn.relu(jnp.matmul(A, h_new))
        key = jax.random.key(seed)
        k_h, k_w0, k_w1 = jax.random.split(key, 3)
        h = jax.random.normal(k_h, (N, E), dtype=jnp.float32)
        adj = jnp.asarray(_build_adj())
        s = 1.0 / np.sqrt(E)
        W0 = jax.random.normal(k_w0, (E, E), dtype=jnp.float32) * s
        b0 = jnp.zeros((E,), dtype=jnp.float32)
        W1 = jax.random.normal(k_w1, (E, E), dtype=jnp.float32) * s
        b1 = jnp.zeros((E,), dtype=jnp.float32)
        return {'h': h, 'adj': adj, 'W0': W0, 'b0': b0, 'W1': W1, 'b1': b1}
    _L0_gnn_all = _L0_gnn_setup()
    _L0_gnn_in = {k: v for k, v in _L0_gnn_all.items() if k in ('W0', 'b0', 'W1', 'b1')}
    del _L0_gnn_all

    def _L1_gnn_setup():
        import jax, jax.numpy as jnp
        import numpy as np
        N = 4096
        D_IN = 128
        D_OUT = 128
        key = jax.random.key(seed)
        k1, k2, k3, k4 = jax.random.split(key, 4)
        x = jax.random.normal(k1, (N, D_IN), dtype=jnp.float32)
        adj = jax.random.uniform(k2, (N, N), dtype=jnp.float32)
        W = jax.random.normal(k3, (D_OUT, D_IN), dtype=jnp.float32) * (1.0 / np.sqrt(D_IN))
        b = jax.random.normal(k4, (D_OUT,), dtype=jnp.float32) * 0.01
        return {'x': x, 'adj': adj, 'W': W, 'b': b}
    _L1_gnn_all = _L1_gnn_setup()
    _L1_gnn_in = {k: v for k, v in _L1_gnn_all.items() if k in ('W', 'b')}
    del _L1_gnn_all
    return {'x': x, 'adj': adj, 'L0_gnn_W0': _L0_gnn_in['W0'], 'L0_gnn_b0': _L0_gnn_in['b0'], 'L0_gnn_W1': _L0_gnn_in['W1'], 'L0_gnn_b1': _L0_gnn_in['b1'], 'L1_gnn_W': _L1_gnn_in['W'], 'L1_gnn_b': _L1_gnn_in['b']}

def reference(x, adj, L0_gnn_W0, L0_gnn_b0, L0_gnn_W1, L0_gnn_b1, L1_gnn_W, L1_gnn_b):
    import jax
    import jax.numpy as jnp

    def _L0_gnn_ref(h, adj, W0, b0, W1, b1):
        import jax, jax.numpy as jnp
        import numpy as np
        N_BLOCKS = 16
        BLOCK = 256
        N = N_BLOCKS * BLOCK
        E = 128
        LAYER_NUM = 2
        NEG = -9000000000000000.0

        def _build_adj():
            filter_num = [BLOCK] * N_BLOCKS
            adj = np.zeros((N, N), dtype=np.float32)
            row = last = filter_num[0]
            for num in filter_num:
                adj[row:row + num, row - last:row] = 1.0
                row += num
                last = num
            np.fill_diagonal(adj, 0.0)
            return adj

        def _gat_layer(h, adj, W, b):
            n, e = h.shape
            att = jnp.matmul(h, h.T) / jnp.sqrt(jnp.asarray(e, h.dtype))
            A = jnp.where(adj > 0, att, jnp.asarray(NEG, h.dtype))
            A = jax.nn.softmax(A, axis=1)
            d = jnp.arange(n)
            A = A * 0.5
            A = A.at[d, d].add(0.5)
            nf1 = jnp.sum(adj[:, 0] != 0)
            mask = d < nf1
            A = jnp.where(mask[:, None], 0.0, A)
            A = A.at[d, d].set(jnp.where(mask, 1.0, A[d, d]))
            h_new = jnp.matmul(h, W.T) + b
            return jax.nn.relu(jnp.matmul(A, h_new))
        x = _gat_layer(h, adj, W0, b0)
        x = _gat_layer(x, adj, W1, b1)
        return x

    def _L1_gnn_ref(x, adj, W, b):
        import jax, jax.numpy as jnp
        import numpy as np
        N = 4096
        D_IN = 128
        D_OUT = 128
        a_hat = adj + jnp.eye(adj.shape[0], dtype=adj.dtype)
        d_inv_sqrt = jnp.sum(a_hat, axis=1) ** (-0.5)
        a_norm = a_hat * d_inv_sqrt[:, None] * d_inv_sqrt[None, :]
        out = a_norm @ x
        out = out @ W.T + b
        return out
    h = jnp.maximum(_layernorm(x, axis=-1), 0.0)
    x = x + _L0_gnn_ref(h, adj, L0_gnn_W0, L0_gnn_b0, L0_gnn_W1, L0_gnn_b1)
    h = jnp.maximum(_layernorm(x, axis=-1), 0.0)
    x = x + _L1_gnn_ref(h, adj, L1_gnn_W, L1_gnn_b)
    return x

_drawn_inputs = setup_inputs


def setup_inputs(seed=0):
    import zlib

    import numpy as np

    out = dict(_drawn_inputs(seed))
    spreads = {'L0_gnn_b0': (0.0, 0.1), 'L0_gnn_b1': (0.0, 0.1)}
    factors = {'L1_gnn_b': 6.759}
    for name, (base, spread) in spreads.items():
        noise = np.random.default_rng([zlib.crc32(name.encode()), seed]).standard_normal(out[name].shape)
        drawn = base * np.exp(spread * noise) if base else spread * noise
        out[name] = jnp.asarray(drawn.astype(out[name].dtype))
    for name, factor in factors.items():
        out[name] = (out[name] * factor).astype(out[name].dtype)
    return out
```

```python
from contextlib import ExitStack

import concourse.bass as bass
from concourse import mybir

ALU = mybir.AluOpType
ACT = mybir.ActivationFunctionType
AX_X = mybir.AxisListType.X
F32 = mybir.dt.float32
F32R = mybir.dt.float32r
BF16 = mybir.dt.bfloat16
U8 = mybir.dt.uint8
U16 = mybir.dt.uint16
I32 = mybir.dt.int32

P = 128
EPS_LN = 1e-5
TINY = 2.0 ** -100
SAFE_SCORE = 60.0


def build(nc, x, adj, W0, b0, W1, b1, Wg, bg, out):
    N, E = x.shape
    assert E == P
    BW = 512
    NB = N // BW
    NJ = N // P
    UNITS = NJ // 2
    RT = BW // P
    CW = 512
    CPR = N // CW
    CHUNKS = RT * CPR
    PAIRS = 2
    AHEAD = 4
    SCALE = float(E) ** -0.5
    EPI = 5
    assert CHUNKS == 2 * UNITS and UNITS % PAIRS == 0 and NB % 2 == 0

    h1T_dram = nc.dram_tensor("h1T_scratch", [P, N], F32, kind="Internal").ap()
    h2T_dram = nc.dram_tensor("h2T_scratch", [P, N], F32, kind="Internal").ap()

    with ExitStack() as ctx:
        base = -(-nc.sbuf_base // 32) * 32
        at = {"next": base}
        SIZE = {F32: 4, F32R: 4, BF16: 2, U8: 1, U16: 2, I32: 4}

        def place(name, shape, dt, offset=None):
            n = SIZE[dt]
            for s in shape[1:]:
                n *= s
            n = -(-n // 32) * 32
            if offset is None:
                offset = at["next"]
                at["next"] += n
            return nc.alloc_sbuf_tensor_at(name, list(shape), dt, offset=offset), offset, offset + n

        adjT, adjT_at, _ = place("adjT", [P, NB, NJ, BW], U8)
        high, high_at, _ = place("high", [P, N], F32R)
        low, low_at, _ = place("low", [P, N], F32R)
        feat, feat_at, _ = place("feat", [P, NJ, P], F32)
        chunk, chunk_at, _ = place("chunk", [P, PAIRS, 2, CW], F32)
        prob, prob_at, _ = place("prob", [P, 2, 2, BW], F32)
        psumR, _, _ = place("prob_sum", [P, BW], F32)
        tA, _, _ = place("tA", [P, BW], F32)
        tB, _, _ = place("tB", [P, BW], F32)
        tC, _, _ = place("tC", [P, BW], F32)
        ident, _, _ = place("ident", [P, P], F32)
        ident_bf, _, _ = place("ident_bf", [P, P], BF16)
        WT_high, _, _ = place("WT_high", [P, 2, P], F32R)
        WT_low, _, _ = place("WT_low", [P, 2, P], F32R)
        row_in_block, _, _ = place("row_in_block", [P, BW], U16)
        junk, _, _ = place("junk", [P, 2, CW], U8)
        deg_part, _, _ = place("deg_part", [P, NB * CHUNKS], F32)
        bias_col, _, _ = place("bias_col", [P, 2], F32)
        tiny_sum, _, _ = place("tiny_sum", [P, 2], F32)
        left_in_block, _, _ = place("left_in_block", [P, NB], F32)
        norm_max, _, _ = place("norm_max", [P, NB], F32)
        all_safe, _, _ = place("all_safe", [P, 1], I32)
        largest, _, _ = place("largest", [P, 1], F32)
        ones, _, work_end = place("ones", [P, P], F32)
        assert work_end <= nc.sbuf_usable_end, work_end - nc.sbuf_usable_end

        scan, _, o = place("scan", [P, 2, BW], F32, offset=chunk_at)
        row_max, _, o = place("row_max", [P, BW], F32, offset=o)
        max_all, _, o = place("max_all", [P, BW], F32, offset=o)
        assert o <= prob_at

        blk = NJ * BW
        x_in, _, _ = place("x_in", [P, NJ, P], F32, offset=adjT_at + 7 * blk)
        h_in, _, _ = place("h_in", [P, NJ, P], F32, offset=adjT_at + 6 * blk)
        o = adjT_at + 5 * blk
        w_in, _, o = place("w_in", [P, 2, P], F32, offset=o)
        stats, _, o = place("stats", [P, NJ, 6], F32, offset=o)
        mean_var, _, o = place("mean_var", [P, NJ, 2], F32, offset=o)
        var_eps, _, o = place("var_eps", [P, NJ], F32, offset=o)
        std, _, o = place("std", [P, NJ], F32, offset=o)
        rstd, _, o = place("rstd", [P, NJ], F32, offset=o)
        col0, _, o = place("col0", [P, N // P], F32, offset=o)
        col0_set, _, o = place("col0_set", [P, N // P], F32, offset=o)
        col0_sum, _, o = place("col0_sum", [P, 1], F32, offset=o)
        first_row, _, o = place("first_row", [P, NB], I32, offset=o)
        first_row_f, _, o = place("first_row_f", [P, NB], F32, offset=o)
        assert o <= adjT_at + 6 * blk

        o = high_at
        x1, _, o = place("x1", [P, NJ, P], F32, offset=o)
        h2T, _, o = place("h2T", [P, NJ, P], F32, offset=o)
        part, _, o = place("part", [P, 3, NJ, P], BF16, offset=o)
        adj_bf, _, o = place("adj_bf", [P, 3, 2, BW], BF16, offset=o)
        aggT, _, o = place("aggT", [P, BW], F32, offset=o)
        res, _, o = place("res", [P, 2, RT, P], F32, offset=o)
        WgT, _, o = place("WgT", [P, P], F32, offset=o)
        bg_all, _, o = place("bg_all", [P, P], F32, offset=o)
        stats2, _, o = place("stats2", [P, NJ, 6], F32, offset=o)
        mean_var2, _, o = place("mean_var2", [P, NJ, 2], F32, offset=o)
        wg_in, _, o = place("wg_in", [P, P], F32, offset=o)
        scal2, _, o = place("scal2", [P, 6, NJ], F32, offset=o)
        deg, var_eps2, std2, rstd2, droot, dinv = (scal2[:, k, :] for k in range(6))
        ident_at = feat_at + 4 * NJ * P + 8 * PAIRS * CW + 4 * 4 * BW + 4 * 4 * BW
        assert o <= ident_at, o - ident_at

        def bank(name, shape):
            return ctx.enter_context(nc.psum_tensor(name, shape, F32))

        pS = bank("pS", [P, 2, 2, BW])
        pAcc = bank("pAcc", [P, 2, BW])
        pMisc = bank("pMisc", [P, BW])
        pT = ctx.enter_context(nc.psum_tensor("pT", [P, 4, 2, P], BF16))

        def sem(name):
            return ctx.enter_context(nc.semaphore(name))

        x_loaded, w_loaded, col0_loaded, bias_loaded = sem("x_loaded"), sem("w_loaded"), sem("col0_loaded"), sem("bias_loaded")
        pool_step, consts_ready = sem("pool_step"), sem("consts_ready")
        v_setup, std_ready, h_ready = sem("v_setup"), sem("std_ready"), sem("h_ready")
        ident_ready = sem("ident_ready")
        hT_turned, high_ready, low_ready = sem("hT_turned"), sem("high_ready"), sem("low_ready")
        w_turned, w_high_ready, w_low_ready = sem("w_turned"), sem("w_high_ready"), sem("w_low_ready")
        feat_made, feat_ready, feat_summed, tiny_ready = sem("feat_made"), sem("feat_ready"), sem("feat_summed"), sem("tiny_ready")
        col0_counted, rows_ready, col0_total = sem("col0_counted"), sem("rows_ready"), sem("col0_total")
        chunk_loaded = [sem(f"chunk_loaded{k}") for k in range(PAIRS)]
        chunk_turned, chunk_summed = sem("chunk_turned"), sem("chunk_summed")
        kept_by_act, kept_by_dve = sem("kept_by_act"), sem("kept_by_dve")
        scores_ready = [sem(f"scores_ready{k}") for k in range(2)]
        exp_ready = [sem(f"exp_ready{k}") for k in range(2)]
        prob_ready = [sem(f"prob_ready{k}") for k in range(2)]
        prob_added = [sem(f"prob_added{k}") for k in range(2)]
        half_added = [sem(f"half_added{k}") for k in range(2)]
        prob_used = [sem(f"prob_used{k}") for k in range(2)]
        own_made = [sem(f"own_made{k}") for k in range(2)]
        own_kept = [sem(f"own_kept{k}") for k in range(2)]
        sum_kept = [sem(f"sum_kept{k}") for k in range(2)]
        den_made = [sem(f"den_made{k}") for k in range(2)]
        epi_step = [sem(f"epi_step{k}") for k in range(2)]
        relu_done = [sem(f"relu_done{k}") for k in range(2)]
        stored = [sem(f"stored{k}") for k in range(2)]
        square_ready, norm_made, norm_read = sem("square_ready"), sem("norm_made"), sem("norm_read")
        h1_loaded = sem("h1_loaded")
        range_known, largest_known = sem("range_known"), sem("largest_known")
        scan_scores, masked, row_max_step = sem("scan_scores"), sem("masked"), sem("row_max_step")
        max_spread, shifted = sem("max_spread"), sem("shifted")
        g_loaded, g_turned, g_added, g_norm, g_std = sem("g_loaded"), sem("g_turned"), sem("g_added"), sem("g_norm"), sem("g_std")
        g_wT, g_wkept, g_part_a, g_part_v, g_hs = sem("g_wT"), sem("g_wkept"), sem("g_part_a"), sem("g_part_v"), sem("g_hs")
        adj_wide, adj_used, agg_kept = sem("adj_wide"), sem("adj_used"), sem("agg_kept")
        res_made, res_ready = sem("res_made"), sem("res_ready")
        res_stored = [sem(f"res_stored{k}") for k in range(2)]
        g_consts = sem("g_consts")

        def is_int(v):
            return isinstance(v, int)

        def wait(eng, s, value):
            if is_int(value):
                if value > 0:
                    eng.wait_ge(s, value)
            else:
                eng.wait_ge(s, value)

        def over_blocks(eng, body):
            body(0, 0, False, True)
            body(1, 1, True, True)
            with eng.Fori(1, NB // 2 - 1) as turn:
                body(turn * 2, 0, True, True)
                body(turn * 2 + 1, 1, True, True)
            body(NB - 2, 0, True, True)
            body(NB - 1, 1, True, False)

        def turned_unit(b, u, has_next):
            if u + AHEAD < UNITS:
                return b, u + AHEAD
            return (b + 1, u + AHEAD - UNITS) if has_next else None

        def one_by_one(eng, body):
            body(0)
            with eng.Fori(1, NB) as b:
                body(b)

        def second_attention(eng, plain, guarded):
            eng.wait_ge(range_known, 1)
            safe = eng.value_load(all_safe[0:1, 0:1], min_val=0, max_val=1)
            with eng.If(safe == 1):
                plain()
            with eng.Else():
                guarded()
            eng.end_ifs()

        def kept_place(b, u):
            q, it = u // 2, 2 * (u % 2)
            if is_int(b):
                return adjT[:, b, 4 * q:4 * q + 4, it * P:(it + 2) * P]
            return adjT[:, bass.ds(b, 1), 4 * q:4 * q + 4, it * P:(it + 2) * P].rearrange("p a t i -> p (a t) i")

        turned = pT[:, :, :, :].rearrange("p t c i -> p t (c i)")

        def adj_unit(b, u):
            if is_int(b):
                return adjT[:, b, 2 * u:2 * u + 2, :]
            return adjT[:, bass.ds(b, 1), 2 * u:2 * u + 2, :].rearrange("p a t i -> p (a t) i")

        def over_pairs(eng, body):
            for par in range(2):
                body(par, par)
            with eng.Fori(1, NB // 2) as turn:
                for par in range(2):
                    body(turn * 2 + par, par)

        ctx.enter_context(nc.allow_non_contiguous_dma(reason="one column of adj"))
        block = ctx.enter_context(nc.Block())

        @block.sync
        def _(sp):
            def load_unit(b, u):
                q, it = u // 2, 2 * (u % 2)
                if u >= PAIRS or not is_int(b):
                    wait(sp, chunk_turned, b * UNITS + u - PAIRS + 1)
                    wait(sp, chunk_summed, b * UNITS + u - PAIRS + 1)
                rows = adj[bass.ds(b * BW + it * P, 2 * P), q * CW:(q + 1) * CW]
                sp.dma_start(chunk[:, u % PAIRS, :, :], rows.rearrange("(c p) j -> p c j", p=P))\
                    .then_inc(chunk_loaded[u % PAIRS], 16)

            for u in range(UNITS):
                load_unit(0, u)
            with sp.Fori(1, NB) as b:
                for u in range(UNITS):
                    load_unit(b, u)
            sp.wait_ge(stored[0], 16 * NB)
            sp.wait_ge(prob_used[0], NB * UNITS)
            sp.dma_start(feat[:, :, :].rearrange("p t j -> p (t j)"), h1T_dram[:, :]).then_inc(h1_loaded, 16)
            sp.wait_ge(stored[1], 16 * NB)
            sp.wait_ge(prob_used[1], NB * UNITS)
            sp.dma_start(h2T[:, :, :].rearrange("p t j -> p (t j)"), h2T_dram[:, :]).then_inc(g_loaded, 16)
            sp.dma_start(x1[:, :, :], x.rearrange("(t p) d -> p t d", p=P)).then_inc(g_loaded, 16)
            sp.dma_start(wg_in[:, :], Wg).then_inc(g_loaded, 16)
            sp.dma_start(bg_all[:, :], bg.rearrange("(a d) -> a d", a=1).broadcast_to([P, P])).then_inc(g_loaded, 16)
            for k in range(2):
                sp.wait_ge(res_stored[k], 16 * (NB // 2))

        @block.gpsimd
        def _(pool):
            nc.gpsimd.memset(ident[:, :], 0.0).then_inc(pool_step, 1)
            nc.gpsimd.memset(ones[:, :], 1.0).then_inc(consts_ready, 1)
            nc.gpsimd.iota(row_in_block[:, :], pattern=[[1, BW]], base=0, channel_multiplier=0).then_inc(consts_ready, 1)
            nc.gpsimd.iota(first_row[:, :], pattern=[[BW, NB]], base=0, channel_multiplier=0).then_inc(consts_ready, 1)
            pool.wait_ge(pool_step, 1)
            nc.gpsimd.affine_select(out=ident[:, :], in_=ident[:, :], compare_op=ALU.not_equal, fill=1.0, base=0,
                                    pattern=[[-1, P]], channel_multiplier=1).then_inc(consts_ready, 1)
            pool.dma_start(col0[:, :], adj[:, 0:1].rearrange("(p t) a -> p (t a)", p=P)).then_inc(col0_loaded, 16)

            def guarded():
                for b in range(NB):
                    wait(pool, shifted, b * UNITS)
                    pool.wait_ge(row_max_step, (b + 1) * UNITS * 2)
                    nc.gpsimd.partition_all_reduce(max_all[:, :], row_max[:, :], P, bass.bass_isa.ReduceOp.max)\
                        .then_inc(max_spread, 1)
            second_attention(pool, lambda: None, guarded)

        @block.scalar
        def _(act):
            act.dma_start(x_in[:, :, :], x.rearrange("(t p) d -> p t d", p=P)).then_inc(x_loaded, 16)
            for k, w in enumerate((W0, W1)):
                act.dma_start(w_in[:, k, :], w).then_inc(w_loaded, 16)
            for k, b in enumerate((b0, b1)):
                act.dma_start(bias_col[:, k:k + 1], b.rearrange("(d a) -> d a", a=1)).then_inc(bias_loaded, 16)

            def keep_unit(b, u):
                act.wait_ge(chunk_turned, b * UNITS + u + 1)
                nc.scalar.activation(kept_place(b, u), turned, ACT.Copy).then_inc(kept_by_act, 1)

            def sum_unit(b, u):
                act.wait_ge(chunk_loaded[u % PAIRS], 16 * (b * (UNITS // PAIRS) + u // PAIRS + 1))
                wait(act, chunk_summed, b * UNITS + u)
                for c in range(2):
                    last = nc.scalar.activation(junk[:, c, :], chunk[:, u % PAIRS, c, :], ACT.Copy,
                                                accum_out=deg_part[:, bass.ds(b * CHUNKS + 2 * u + c, 1)])
                last.then_inc(chunk_summed, 1)

            def feat_copies(L):
                for grp in range(NJ // 4):
                    act.wait_ge(feat_made, L * (NJ // 4) + grp + 1)
                    nc.scalar.activation(feat[:, 4 * grp:4 * grp + 4, :],
                                         pS[:, (grp // 2) % 2, grp % 2, :].rearrange("p (t d) -> p t d", t=4),
                                         ACT.Copy).then_inc(feat_ready, 1)

            sum_unit(0, 0)
            keep_unit(0, 0)
            sum_unit(0, 1)
            act.wait_ge(v_setup, 1)
            nc.scalar.activation(std[:, :], var_eps[:, :], ACT.Sqrt).then_inc(std_ready, 1)
            for k in range(2):
                act.wait_ge(w_turned, 2)
                nc.scalar.activation(WT_high[:, k, :], pMisc[:, k * P:(k + 1) * P], ACT.Copy).then_inc(w_high_ready, 1)
            for grp in range(NJ // 4):
                act.wait_ge(hT_turned, grp + 1)
                nc.scalar.activation(high[:, grp * BW:(grp + 1) * BW], pS[:, (grp // 2) % 2, grp % 2, :],
                                     ACT.Relu).then_inc(high_ready, 1)
            feat_copies(0)
            sum_unit(0, 2)
            keep_unit(0, 2)
            sum_unit(0, 3)

            def epi_own(L, b):
                act.wait_ge(own_made[L], b + 1)
                wait(act, epi_step[L], b * EPI)
                nc.scalar.activation(tB[:, :], pMisc[:, :], ACT.Copy).then_inc(own_kept[L], 1)

            def epi_relu(L, b):
                act.wait_ge(epi_step[L], b * EPI + EPI)
                nc.scalar.activation(tC[:, :], tA[:, :], ACT.Relu, bias=bias_col[:, L:L + 1]).then_inc(relu_done[L], 1)
                act.wait_ge(relu_done[L], b + 1)
                dst = (h1T_dram, h2T_dram)[L]
                act.dma_start(dst[:, bass.ds(b * BW, BW)], tC[:, :]).then_inc(stored[L], 16)
                if L == 0:
                    nc.scalar.activation(tA[:, :], tC[:, :], ACT.Square).then_inc(square_ready, 1)

            def attention(L):
                def body(b, par, has_prev, has_next):
                    for u in range(UNITS):
                        g = b * UNITS + u
                        act.wait_ge(scores_ready[L], g + 1)
                        if not (is_int(b) and b == 0 and u < 2):
                            wait(act, prob_used[L], g - 1)
                            wait(act, prob_added[L], g - 1)
                        nc.scalar.activation(prob[:, u % 2, :, :], pS[:, u % 2, :, :], ACT.Exp,
                                             scale=SCALE).then_inc(exp_ready[L], 1)
                        ahead = turned_unit(b, u, has_next)
                        if L == 0 and ahead:
                            if u % 2 == 0:
                                keep_unit(*ahead)
                            sum_unit(*ahead)
                        if has_prev and u == 1:
                            epi_own(L, b - 1)
                        if has_prev and u == 9:
                            epi_relu(L, b - 1)
                over_blocks(act, body)
                epi_own(L, NB - 1)
                epi_relu(L, NB - 1)

            act.wait_ge(bias_loaded, 32)
            attention(0)
            act.wait_ge(h1_loaded, 16)
            for grp in range(NJ // 4):
                nc.scalar.activation(high[:, grp * BW:(grp + 1) * BW],
                                     feat[:, 4 * grp:4 * grp + 4, :].rearrange("p t j -> p (t j)"),
                                     ACT.Copy).then_inc(high_ready, 1)
            act.wait_ge(low_ready, 2 * (NJ // 4))
            feat_copies(1)

            def guarded():
                def body(b):
                    for u in range(UNITS):
                        act.wait_ge(shifted, b * UNITS + u + 1)
                        nc.scalar.activation(prob[:, u % 2, :, :], prob[:, u % 2, :, :], ACT.Exp,
                                             scale=SCALE).then_inc(exp_ready[1], 1)
                    epi_own(1, b)
                    epi_relu(1, b)
                one_by_one(act, body)
            second_attention(act, lambda: attention(1), guarded)

            act.wait_ge(g_norm, 1)
            nc.scalar.activation(std2, var_eps2, ACT.Sqrt).then_inc(g_std, 1)
            nc.scalar.activation(droot, deg, ACT.Sqrt).then_inc(g_std, 1)
            act.wait_ge(g_wT, 1)
            nc.scalar.activation(WgT[:, :], pMisc[:, 0:P], ACT.Copy).then_inc(g_wkept, 1)
            for grp in range(4):
                sl = slice(grp * NJ // 4, (grp + 1) * NJ // 4)
                act.wait_ge(g_hs, grp + 1)
                nc.scalar.activation(part[:, 0, sl, :], h2T[:, sl, :], ACT.Copy).then_inc(g_part_a, 1)
                act.wait_ge(g_part_v, 2 * grp + 1)
                nc.scalar.activation(part[:, 1, sl, :], h2T[:, sl, :], ACT.Copy).then_inc(g_part_a, 1)

            def body(b, par):
                act.wait_ge(adj_used, (b + 1) * UNITS)
                wait(act, res_made, b)
                nc.scalar.activation(aggT[:, :], pAcc[:, par, :], ACT.Copy).then_inc(agg_kept, 1)
                act.wait_ge(res_ready, b + 1)
                act.dma_start(out[bass.ds(b * BW, BW), :].rearrange("(t p) d -> p t d", p=P),
                              res[:, par, :, :]).then_inc(res_stored[par], 16)
            over_pairs(act, body)

        @block.vector
        def _(dve):
            def keep_unit(b, u):
                dve.wait_ge(chunk_turned, b * UNITS + u + 1)
                nc.vector.tensor_copy(kept_place(b, u), turned).then_inc(kept_by_dve, 1)

            dve.wait_ge(consts_ready, 4)
            nc.vector.tensor_copy(ident_bf[:, :], ident[:, :]).then_inc(ident_ready, 1)
            dve.wait_ge(x_loaded, 16)
            for t in range(NJ):
                nc.vector.bn_stats(stats[:, t, :], x_in[:, t, :]).then_inc(h_ready, 1)
            for t in range(NJ):
                dve.wait_ge(h_ready, t + 1)
                nc.vector.bn_aggr(mean_var[:, t, :], stats[:, t, :]).then_inc(h_ready, 1)
            dve.wait_ge(h_ready, 2 * NJ)
            nc.vector.tensor_scalar(var_eps[:, :], mean_var[:, :, 1], EPS_LN, None, ALU.add).then_inc(v_setup, 1)
            dve.wait_ge(std_ready, 1)
            nc.vector.reciprocal(rstd[:, :], std[:, :]).then_inc(v_setup, 1)
            dve.wait_ge(v_setup, 2)
            for t in range(NJ):
                nc.vector.tensor_scalar(h_in[:, t, :], x_in[:, t, :], mean_var[:, t, 0:1], rstd[:, t:t + 1],
                                        ALU.subtract, ALU.mult).then_inc(h_ready, 1)
            keep_unit(0, 1)
            for k in range(2):
                dve.wait_ge(w_high_ready, 2)
                nc.vector.tensor_tensor(WT_low[:, k, :], pMisc[:, k * P:(k + 1) * P],
                                        WT_high[:, k, :].bitcast(F32), ALU.subtract).then_inc(w_low_ready, 1)
            for grp in range(NJ // 4):
                cols = slice(grp * BW, (grp + 1) * BW)
                dve.wait_ge(high_ready, grp + 1)
                nc.vector.scalar_tensor_tensor(out=low[:, cols], in0=pS[:, (grp // 2) % 2, grp % 2, :], scalar=0.0,
                                               in1=high[:, cols].bitcast(F32), op0=ALU.max,
                                               op1=ALU.subtract).then_inc(low_ready, 1)
            dve.wait_ge(col0_loaded, 16)
            nc.vector.tensor_scalar(col0_set[:, :], col0[:, :], 0.0, None, ALU.not_equal).then_inc(v_setup, 1)
            dve.wait_ge(v_setup, 3)
            nc.vector.tensor_reduce(col0_sum[:, :], col0_set[:, :], AX_X, ALU.add).then_inc(col0_counted, 1)
            dve.wait_ge(consts_ready, 4)
            nc.vector.tensor_copy(first_row_f[:, :], first_row[:, :]).then_inc(v_setup, 1)
            dve.wait_ge(v_setup, 4)
            dve.wait_ge(col0_total, 1)
            nc.vector.tensor_scalar(left_in_block[:, :], first_row_f[:, :], -1.0, pMisc[:, 2 * P:2 * P + 1],
                                    ALU.mult, ALU.add).then_inc(rows_ready, 1)
            dve.wait_ge(feat_summed, 1)
            nc.vector.tensor_scalar(tiny_sum[:, 0:1], pMisc[:, 2 * P + 2:2 * P + 3], TINY, None,
                                    ALU.mult).then_inc(tiny_ready, 1)
            dve.wait_ge(tiny_ready, 1)
            dve.wait_ge(rows_ready, 1)
            keep_unit(0, 3)

            def epilogue(L, b, par, step):
                s = epi_step[L]
                if step == 0:
                    dve.wait_ge(den_made[L], b + 1)
                    wait(dve, stored[L], b * 16)
                    if L == 0:
                        wait(dve, square_ready, b)
                    nc.vector.reciprocal(tC[:, :], pMisc[:, :]).then_inc(s, 1)
                elif step == 1:
                    dve.wait_ge(s, b * EPI + 1)
                    dve.wait_ge(prob_used[L], b * UNITS + UNITS)
                    nc.vector.scalar_tensor_tensor(out=tA[:, :], in0=pAcc[:, par, :], scalar=tiny_sum[:, L:L + 1],
                                                   in1=tC[:, :], op0=ALU.add, op1=ALU.mult).then_inc(s, 1)
                elif step == 2:
                    dve.wait_ge(s, b * EPI + 2)
                    dve.wait_ge(own_kept[L], b + 1)
                    nc.vector.tensor_tensor(tA[:, :], tA[:, :], tB[:, :], ALU.subtract).then_inc(s, 1)
                elif step == 3:
                    dve.wait_ge(s, b * EPI + 3)
                    left = left_in_block[:, b:b + 1] if is_int(b) else left_in_block[:, bass.ds(b, 1)]
                    nc.vector.scalar_tensor_tensor(out=tA[:, :], in0=row_in_block[:, :], scalar=left, in1=tA[:, :],
                                                   op0=ALU.is_ge, op1=ALU.mult).then_inc(s, 1)
                elif step == 4:
                    dve.wait_ge(s, b * EPI + 4)
                    nc.vector.scalar_tensor_tensor(out=tA[:, :], in0=tA[:, :], scalar=0.5, in1=tB[:, :],
                                                   op0=ALU.mult, op1=ALU.add).then_inc(s, 1)

            def epi_norm(b):
                dve.wait_ge(norm_made, b + 1)
                dst = norm_max[:, b:b + 1] if is_int(b) else norm_max[:, bass.ds(b, 1)]
                nc.vector.tensor_reduce(dst, pMisc[:, :], AX_X, ALU.max).then_inc(norm_read, 1)

            def attention(L):
                def body(b, par, has_prev, has_next):
                    for u in range(UNITS):
                        if L == 0 and u % 2 == 0:
                            dve.wait_ge(kept_by_act, b * (UNITS // 2) + u // 2 + 1)
                            dve.wait_ge(kept_by_dve, b * (UNITS // 2) + u // 2 + 1)
                        g = b * UNITS + u
                        pr = prob[:, u % 2, :, :]
                        a = adj_unit(b, u)
                        dve.wait_ge(exp_ready[L], g + 1)
                        nc.vector.tensor_tensor(pr, pr, a, ALU.mult).then_inc(prob_ready[L], 1)
                        ahead = turned_unit(b, u, has_next)
                        if L == 0 and ahead and u % 2 == 1:
                            keep_unit(*ahead)
                        add_unit(L, b, u)
                        if has_prev and 4 <= u < 4 + EPI:
                            epilogue(L, b - 1, 1 - par, u - 4)
                        if has_prev and u == 12 and L == 0:
                            epi_norm(b - 1)
                    keep_sum(L, b)

                over_blocks(dve, body)
                for step in range(EPI):
                    epilogue(L, NB - 1, 1, step)
                if L == 0:
                    epi_norm(NB - 1)

            def add_unit(L, b, u):
                g = b * UNITS + u
                pr = prob[:, u % 2, :, :]
                dve.wait_ge(prob_ready[L], g + 1)
                if u == 0:
                    wait(dve, sum_kept[L], b)
                    nc.vector.tensor_scalar(psumR[:, :], pr[:, 0, :], (N // P) * TINY, None,
                                            ALU.add).then_inc(half_added[L], 1)
                else:
                    dve.wait_ge(prob_added[L], g)
                    nc.vector.tensor_tensor(psumR[:, :], psumR[:, :], pr[:, 0, :], ALU.add).then_inc(half_added[L], 1)
                dve.wait_ge(half_added[L], g + 1)
                nc.vector.tensor_tensor(psumR[:, :], psumR[:, :], pr[:, 1, :], ALU.add).then_inc(prob_added[L], 1)

            def keep_sum(L, b):
                dve.wait_ge(prob_added[L], b * UNITS + UNITS)
                if L == 0:
                    wait(dve, norm_made, b)
                else:
                    wait(dve, relu_done[L], b)
                nc.vector.tensor_copy(tA[:, :], psumR[:, :]).then_inc(sum_kept[L], 1)

            def guarded():
                def body(b):
                    for u in range(UNITS):
                        g = b * UNITS + u
                        dve.wait_ge(scan_scores, g + 1)
                        wait(dve, row_max_step, 2 * g)
                        nc.vector.tensor_tensor(scan[:, :, :], pS[:, u % 2, :, :], adj_unit(b, u),
                                                ALU.mult).then_inc(masked, 1)
                        dve.wait_ge(masked, g + 1)
                        if u == 0:
                            wait(dve, max_spread, b)
                            nc.vector.tensor_copy(row_max[:, :], scan[:, 0, :]).then_inc(row_max_step, 1)
                        else:
                            nc.vector.tensor_tensor(row_max[:, :], row_max[:, :], scan[:, 0, :],
                                                    ALU.max).then_inc(row_max_step, 1)
                        dve.wait_ge(row_max_step, 2 * g + 1)
                        nc.vector.tensor_tensor(row_max[:, :], row_max[:, :], scan[:, 1, :],
                                                ALU.max).then_inc(row_max_step, 1)
                        dve.wait_ge(row_max_step, 2 * g + 2)
                    dve.wait_ge(max_spread, b + 1)
                    for u in range(UNITS):
                        g = b * UNITS + u
                        pr = prob[:, u % 2, :, :]
                        dve.wait_ge(scores_ready[1], g + 1)
                        if not (is_int(b) and u < 2):
                            dve.wait_ge(prob_used[1], g - 1)
                            dve.wait_ge(prob_added[1], g - 1)
                        for h in range(2):
                            last = nc.vector.tensor_tensor(pr[:, h, :], pS[:, u % 2, h, :], max_all[:, :],
                                                           ALU.subtract)
                        last.then_inc(shifted, 1)
                        dve.wait_ge(exp_ready[1], g + 1)
                        nc.vector.scalar_tensor_tensor(out=pr, in0=pr, scalar=3e38, in1=adj_unit(b, u),
                                                       op0=ALU.min, op1=ALU.mult).then_inc(prob_ready[1], 1)
                        add_unit(1, b, u)
                    keep_sum(1, b)
                    for step in range(EPI):
                        epilogue(1, b, 0, step)
                one_by_one(dve, body)

            attention(0)
            dve.wait_ge(norm_read, NB)
            nc.vector.tensor_reduce(largest[:, :], norm_max[:, :], AX_X, ALU.max).then_inc(largest_known, 1)
            dve.wait_ge(largest_known, 1)
            nc.vector.tensor_scalar(all_safe[:, :], largest[:, :], SAFE_SCORE / SCALE, None,
                                    ALU.is_le).then_inc(range_known, 1)
            dve.wait_ge(h1_loaded, 16)
            for grp in range(NJ // 4):
                cols = slice(grp * BW, (grp + 1) * BW)
                dve.wait_ge(high_ready, NJ // 4 + grp + 1)
                nc.vector.tensor_tensor(low[:, cols], feat[:, 4 * grp:4 * grp + 4, :].rearrange("p t j -> p (t j)"),
                                        high[:, cols].bitcast(F32), ALU.subtract).then_inc(low_ready, 1)
            dve.wait_ge(feat_summed, 2)
            nc.vector.tensor_scalar(tiny_sum[:, 1:2], pMisc[:, 2 * P + 2:2 * P + 3], TINY, None,
                                    ALU.mult).then_inc(tiny_ready, 1)
            dve.wait_ge(tiny_ready, 2)
            second_attention(dve, lambda: attention(1), guarded)

            n = 0
            dve.wait_ge(g_loaded, 64)
            for grp in range(NJ // 4):
                sl = slice(4 * grp, 4 * grp + 4)
                dve.wait_ge(g_turned, grp + 1)
                nc.vector.tensor_tensor(x1[:, sl, :], x1[:, sl, :],
                                        pS[:, (grp // 2) % 2, grp % 2, :].rearrange("p (t d) -> p t d", t=4),
                                        ALU.add).then_inc(g_added, 1)
            for t in range(NJ):
                dve.wait_ge(g_added, t // 4 + 1)
                nc.vector.bn_stats(stats2[:, t, :], x1[:, t, :]).then_inc(v_setup, 1)
            for t in range(NJ):
                dve.wait_ge(v_setup, 4 + t + 1)
                nc.vector.bn_aggr(mean_var2[:, t, :], stats2[:, t, :]).then_inc(v_setup, 1)
            n = 4 + 2 * NJ
            nc.vector.tensor_reduce(deg.rearrange("p (b t) -> p b t", t=RT),
                                    deg_part[:, :].rearrange("p (b q t) -> p b t q", q=CPR, t=RT), AX_X,
                                    ALU.add).then_inc(v_setup, 1)
            dve.wait_ge(v_setup, n + 1)
            nc.vector.tensor_scalar(var_eps2, mean_var2[:, :, 1], EPS_LN, None, ALU.add).then_inc(v_setup, 1)
            nc.vector.tensor_scalar(deg, deg, 1.0, None, ALU.add).then_inc(v_setup, 1)
            dve.wait_ge(v_setup, n + 3)
            nc.vector.tensor_copy(deg, deg).then_inc(g_norm, 1)
            dve.wait_ge(g_std, 2)
            nc.vector.reciprocal(rstd2, std2).then_inc(v_setup, 1)
            nc.vector.reciprocal(dinv, droot).then_inc(v_setup, 1)
            dve.wait_ge(v_setup, n + 5)
            dve.wait_ge(g_turned, NJ // 4)
            n += 5
            for grp in range(4):
                tiles = range(grp * NJ // 4, (grp + 1) * NJ // 4)
                for t in tiles:
                    nc.vector.tensor_scalar(h2T[:, t, :], x1[:, t, :], mean_var2[:, t, 0:1], rstd2[:, t:t + 1],
                                            ALU.subtract, ALU.mult).then_inc(v_setup, 1)
                for t in tiles:
                    n += 1
                    dve.wait_ge(v_setup, n)
                    last = nc.vector.tensor_scalar(h2T[:, t, :], h2T[:, t, :], 0.0, dinv[:, t:t + 1],
                                                   ALU.max, ALU.mult)
                    last.then_inc(g_hs if t == tiles[-1] else v_setup, 1)
                n += len(tiles) - 1
                for t in tiles:
                    nc.vector.tensor_tensor(x1[:, t, :], x1[:, t, :], bg_all[:, :], ALU.add).then_inc(v_setup, 1)
                n += len(tiles)
                sl = slice(tiles[0], tiles[-1] + 1)
                for k in range(2):
                    dve.wait_ge(g_part_a, 2 * grp + k + 1)
                    dst = h2T[:, sl, :] if k == 0 else part[:, 2, sl, :]
                    nc.vector.tensor_tensor(dst, h2T[:, sl, :], part[:, k, sl, :], ALU.subtract).then_inc(g_part_v, 1)

            def body(b, par):
                for u in range(UNITS):
                    g = b * UNITS + u
                    if not (is_int(b) and b == 0 and u < 2):
                        wait(dve, adj_used, g - 1)
                    a = adj_unit(b, u)
                    nc.vector.tensor_copy(adj_bf[:, u % 2, :, :], a).then_inc(adj_wide, 1)
                    if u == 2 and not (is_int(b) and b == 0):
                        finish(b - 1, 1 - par)

            def finish(b, par):
                dve.wait_ge(res_made, b + 1)
                if not (is_int(b) and b < 2):
                    dve.wait_ge(res_stored[par], (b - par) * 8)
                for t in range(RT):
                    row = b * RT + t
                    last = nc.vector.scalar_tensor_tensor(
                        out=res[:, par, t, :], in0=pMisc[:, t * P:(t + 1) * P], scalar=scal2[:, 5, bass.ds(row, 1)],
                        in1=x1[:, bass.ds(row, 1), :].rearrange("p a d -> p (a d)"), op0=ALU.mult, op1=ALU.add)
                last.then_inc(res_ready, 1)
            over_pairs(dve, body)
            finish(NB - 1, 1)

        @block.tensor
        def _(pe):
            pe.wait_ge(consts_ready, 4)

            def turn_unit(b, u):
                pe.wait_ge(chunk_loaded[u % PAIRS], 16 * (b * (UNITS // PAIRS) + u // PAIRS + 1))
                if u % 2:
                    pe.wait_ge(kept_by_act, b * (UNITS // 2) + u // 2 + 1)
                else:
                    wait(pe, kept_by_dve, b * (UNITS // 2) + u // 2)
                for c in range(2):
                    upper = chunk[:, u % PAIRS, c, :].bitcast(BF16).rearrange("p (j two) -> p j two", two=2)[:, :, 1]
                    for m in range(4):
                        mm = nc.tensor.transpose(pT[:, m, c, :], upper[:, m * P:(m + 1) * P], ident_bf[:, :])
                mm.then_inc(chunk_turned, 1)

            def product3(dst, a_high, a_low, b_high, b_low):
                nc.tensor.matmul(dst, a_high, b_high, start=True, stop=False)
                nc.tensor.matmul(dst, a_high, b_low, start=False, stop=False)
                return nc.tensor.matmul(dst, a_low, b_high, start=False, stop=True)

            def make_feat(L):
                for grp in range(NJ // 4):
                    pe.wait_ge(low_ready, L * (NJ // 4) + (grp + 1 if L == 0 else NJ // 4))
                    if grp >= 4:
                        pe.wait_ge(feat_ready, L * (NJ // 4) + grp - 3)
                    else:
                        pe.wait_ge(low_ready, L * (NJ // 4) + (grp + 5 if L == 0 else NJ // 4))
                    for t in range(4 * grp, 4 * grp + 4):
                        mm = product3(pS[:, (grp // 2) % 2, grp % 2, (t % 4) * P:(t % 4 + 1) * P],
                                      high[:, t * P:(t + 1) * P], low[:, t * P:(t + 1) * P],
                                      WT_high[:, L, :], WT_low[:, L, :])
                    mm.then_inc(feat_made, 1)
                pe.wait_ge(feat_ready, (L + 1) * (NJ // 4))
                pe.wait_ge(rows_ready, 1)
                for t in range(NJ):
                    mm = nc.tensor.matmul(pMisc[:, 2 * P + 2:2 * P + 3], feat[:, t, :], ones[:, 0:1],
                                          start=(t == 0), stop=(t == NJ - 1))
                mm.then_inc(feat_summed, 1)

            pe.wait_ge(ident_ready, 1)
            turn_unit(0, 0)
            turn_unit(0, 1)
            pe.wait_ge(w_loaded, 32)
            for k in range(2):
                nc.tensor.transpose(pMisc[:, k * P:(k + 1) * P], w_in[:, k, :], ident[:, :]).then_inc(w_turned, 1)
            for grp in range(NJ // 4):
                pe.wait_ge(h_ready, 2 * NJ + 4 * grp + 4)
                if grp >= 4:
                    pe.wait_ge(low_ready, grp - 3)
                for t in range(4 * grp, 4 * grp + 4):
                    mm = nc.tensor.transpose(pS[:, (grp // 2) % 2, grp % 2, (t % 4) * P:(t % 4 + 1) * P],
                                             h_in[:, t, :], ident[:, :])
                mm.then_inc(hT_turned, 1)
            pe.wait_ge(w_low_ready, 2)
            pe.wait_ge(col0_counted, 1)
            nc.tensor.matmul(pMisc[:, 2 * P:2 * P + 1], ones[:, :], col0_sum[:, :], start=True, stop=True)\
                .then_inc(col0_total, 1)
            make_feat(0)
            turn_unit(0, 2)
            turn_unit(0, 3)

            def unit_scores(b, u):
                rows = bass.ds(b * BW, BW)
                for h in range(2):
                    t = 2 * u + h
                    mm = product3(pS[:, u % 2, h, :], high[:, t * P:(t + 1) * P], low[:, t * P:(t + 1) * P],
                                  high[:, rows], low[:, rows])
                return mm

            def scores(L, b, u):
                if not (is_int(b) and b == 0 and u < 2):
                    pe.wait_ge(exp_ready[L], b * UNITS + u - 1)
                unit_scores(b, u).then_inc(scores_ready[L], 1)

            def own(L, b):
                if L == 0:
                    wait(pe, norm_read, b)
                else:
                    wait(pe, epi_step[L], b * EPI)
                rows = bass.ds(b * BW, BW)
                product3(pMisc[:, :], WT_high[:, L, :], WT_low[:, L, :], high[:, rows], low[:, rows])\
                    .then_inc(own_made[L], 1)

            def denominator(L, b):
                pe.wait_ge(own_kept[L], b + 1)
                pe.wait_ge(sum_kept[L], b + 1)
                nc.tensor.matmul(pMisc[:, :], ones[:, :], tA[:, :], start=True, stop=True).then_inc(den_made[L], 1)

            def norms(b):
                pe.wait_ge(square_ready, b + 1)
                nc.tensor.matmul(pMisc[:, :], ones[:, :], tA[:, :], start=True, stop=True).then_inc(norm_made, 1)

            def mix(L, b, par, u):
                pe.wait_ge(prob_ready[L], b * UNITS + u + 1)
                for h in range(2):
                    mm = nc.tensor.matmul(pAcc[:, par, :], feat[:, 2 * u + h, :], prob[:, u % 2, h, :],
                                          start=(u == 0 and h == 0), stop=(u == UNITS - 1 and h == 1))
                mm.then_inc(prob_used[L], 1)

            def attention(L):
                def body(b, par, has_prev, has_next):
                    for u in range(UNITS):
                        ahead = turned_unit(b, u, has_next)
                        if L == 0 and ahead:
                            turn_unit(*ahead)
                        if u < UNITS - 1:
                            scores(L, b, u + 1)
                        elif has_next:
                            scores(L, b + 1, 0)
                        if has_prev and u == 1:
                            own(L, b - 1)
                        if has_prev and u == 3:
                            denominator(L, b - 1)
                        if has_prev and u == 11 and L == 0:
                            norms(b - 1)
                        if u == 0 and not (is_int(b) and b < 2):
                            pe.wait_ge(epi_step[L], (b - 1) * EPI)
                        mix(L, b, par, u)

                pe.wait_ge(tiny_ready, L + 1)
                scores(L, 0, 0)
                over_blocks(pe, body)
                own(L, NB - 1)
                denominator(L, NB - 1)
                if L == 0:
                    norms(NB - 1)

            def guarded():
                def body(b):
                    for u in range(UNITS):
                        g = b * UNITS + u
                        if u < 2:
                            wait(pe, shifted, b * UNITS)
                        else:
                            pe.wait_ge(row_max_step, 2 * g - 2)
                        unit_scores(b, u).then_inc(scan_scores, 1)
                    pe.wait_ge(max_spread, b + 1)
                    for u in range(UNITS):
                        if u >= 2:
                            pe.wait_ge(shifted, b * UNITS + u - 1)
                        unit_scores(b, u).then_inc(scores_ready[1], 1)
                        if u >= 1:
                            if u == 1:
                                wait(pe, epi_step[1], b * EPI)
                            mix(1, b, 0, u - 1)
                    mix(1, b, 0, UNITS - 1)
                    own(1, b)
                    denominator(1, b)
                one_by_one(pe, body)

            attention(0)
            pe.wait_ge(norm_read, NB)
            make_feat(1)
            pe.wait_ge(tiny_ready, 2)
            second_attention(pe, lambda: attention(1), guarded)

            pe.wait_ge(g_loaded, 64)
            pe.wait_ge(exp_ready[1], NB * UNITS)
            for grp in range(NJ // 4):
                if grp >= 4:
                    pe.wait_ge(g_added, grp - 3)
                for t in range(4 * grp, 4 * grp + 4):
                    mm = nc.tensor.transpose(pS[:, (grp // 2) % 2, grp % 2, (t % 4) * P:(t % 4 + 1) * P],
                                             h2T[:, t, :], ident[:, :])
                mm.then_inc(g_turned, 1)
            pe.wait_ge(epi_step[1], NB * EPI)
            nc.tensor.transpose(pMisc[:, 0:P], wg_in[:, :], ident[:, :]).then_inc(g_wT, 1)
            pe.wait_ge(g_wkept, 1)
            pe.wait_ge(g_part_v, 8)
            pe.wait_ge(g_part_a, 8)

            def body(b, par):
                for u in range(UNITS):
                    pe.wait_ge(adj_wide, b * UNITS + u + 1)
                    if u == 0 and not (is_int(b) and b < 2):
                        pe.wait_ge(agg_kept, b - 1)
                    if u == UNITS - 1:
                        for t in range(RT):
                            for k in range(3):
                                own = part[:, k, bass.ds(b * RT + t, 1), :].rearrange("p a d -> p (a d)")
                                nc.tensor.matmul(pAcc[:, par, t * P:(t + 1) * P], own, ident_bf[:, :], start=False,
                                                 stop=False, skip_group_check=True)
                    for h in range(2):
                        for k in range(3):
                            mm = nc.tensor.matmul(pAcc[:, par, :], part[:, k, 2 * u + h, :], adj_bf[:, u % 2, h, :],
                                                  start=(u == 0 and h == 0 and k == 0),
                                                  stop=(u == UNITS - 1 and h == 1 and k == 2))
                    mm.then_inc(adj_used, 1)
                    if u == 1 and not (is_int(b) and b == 0):
                        project(b - 1)

            def project(b):
                pe.wait_ge(agg_kept, b + 1)
                wait(pe, res_ready, b)
                for t in range(RT):
                    mm = nc.tensor.matmul(pMisc[:, t * P:(t + 1) * P], aggT[:, t * P:(t + 1) * P], WgT[:, :],
                                          start=True, stop=True)
                mm.then_inc(res_made, 1)
            over_pairs(pe, body)
            project(NB - 1)


_INS = ['x', 'adj', 'L0_gnn_W0', 'L0_gnn_b0', 'L0_gnn_W1', 'L0_gnn_b1', 'L1_gnn_W', 'L1_gnn_b']
_OUTS = [((4096, 128), 'float32')]


def kernel(**inputs):
    import numpy as _np
    import concourse.bacc as _bacc
    from concourse import mybir as _mybir
    from concourse.bass_utils import run_bass_kernel_spmd as _run

    nc = _bacc.Bacc("TRN2", target_bir_lowering=False, num_devices=1)
    arrays, args = {}, []
    for name in _INS:
        a = _np.ascontiguousarray(inputs[name])
        arrays[f"in_{name}_dram"] = a
        args.append(nc.dram_tensor(f"in_{name}_dram", a.shape, _mybir.dt.from_np(a.dtype), kind="ExternalInput").ap())
    for i, (shape, dtype) in enumerate(_OUTS):
        dt = _mybir.dt.from_np(_np.dtype(dtype))
        args.append(nc.dram_tensor(f"out_{i}_dram", shape, dt, kind="ExternalOutput").ap())
    build(nc, *args)
    r = _run(nc, [arrays], core_ids=[0])
    return r.results[0]["out_0_dram"]
```

```python
from contextlib import ExitStack

import concourse.bass as bass
from concourse import mybir

ALU = mybir.AluOpType
ACT = mybir.ActivationFunctionType
AX_X = mybir.AxisListType.X
F32 = mybir.dt.float32
F32R = mybir.dt.float32r
BF16 = mybir.dt.bfloat16
U8 = mybir.dt.uint8
U16 = mybir.dt.uint16
I32 = mybir.dt.int32

P = 128
EPS_LN = 1e-5
TINY = 2.0 ** -100
SAFE_SCORE = 60.0


def build(nc, x, adj, W0, b0, W1, b1, Wg, bg, out):
    N, E = x.shape
    assert E == P
    BW = 512
    NB = N // BW
    NJ = N // P
    UNITS = NJ // 2
    RT = BW // P
    CW = 512
    CPR = N // CW
    CHUNKS = RT * CPR
    PAIRS = 2
    AHEAD = 4
    SCALE = float(E) ** -0.5
    EPI = 5
    assert CHUNKS == 2 * UNITS and UNITS % PAIRS == 0 and NB % 2 == 0

    h1T_dram = nc.dram_tensor("h1T_scratch", [P, N], F32, kind="Internal").ap()
    x1_dram = nc.dram_tensor("x1_scratch", [N, E], F32, kind="Internal").ap()

    with ExitStack() as ctx:
        base = -(-nc.sbuf_base // 32) * 32
        at = {"next": base}
        SIZE = {F32: 4, F32R: 4, BF16: 2, U8: 1, U16: 2, I32: 4}

        def place(name, shape, dt, offset=None):
            n = SIZE[dt]
            for s in shape[1:]:
                n *= s
            n = -(-n // 32) * 32
            if offset is None:
                offset = at["next"]
                at["next"] += n
            return nc.alloc_sbuf_tensor_at(name, list(shape), dt, offset=offset), offset, offset + n

        adjT, adjT_at, _ = place("adjT", [P, NB, NJ, BW], U8)
        high, high_at, _ = place("high", [P, N], F32R)
        low, low_at, _ = place("low", [P, N], F32R)
        feat, feat_at, _ = place("feat", [P, NJ, P], F32)
        chunk, chunk_at, _ = place("chunk", [P, PAIRS, 2, CW], F32)
        prob, prob_at, _ = place("prob", [P, 2, 2, BW], F32)
        psumR, _, _ = place("prob_sum", [P, BW], F32)
        tA, _, _ = place("tA", [P, BW], F32)
        tB, _, _ = place("tB", [P, BW], F32)
        tC, _, _ = place("tC", [P, BW], F32)
        ident, _, _ = place("ident", [P, P], F32)
        ident_bf, _, _ = place("ident_bf", [P, P], BF16)
        WT_high, _, _ = place("WT_high", [P, 2, P], F32R)
        WT_low, _, _ = place("WT_low", [P, 2, P], F32R)
        row_in_block, _, _ = place("row_in_block", [P, BW], U16)
        junk, _, _ = place("junk", [P, 2, CW], U8)
        deg_part, _, _ = place("deg_part", [P, NB * CHUNKS], F32)
        bias_col, _, _ = place("bias_col", [P, 2], F32)
        tiny_sum, _, _ = place("tiny_sum", [P, 2], F32)
        left_in_block, _, _ = place("left_in_block", [P, NB], F32)
        norm_max, _, _ = place("norm_max", [P, NB], F32)
        all_safe, _, _ = place("all_safe", [P, 1], I32)
        largest, _, _ = place("largest", [P, 1], F32)
        WgT, _, _ = place("WgT", [P, P], F32)
        bg_all, _, _ = place("bg_all", [P, P], F32)
        ones, _, work_end = place("ones", [P, P], F32)
        assert work_end <= nc.sbuf_usable_end, work_end - nc.sbuf_usable_end

        scan = prob[:, 0, :, :]
        row_max, max_all = tA, tB

        x_block, _, o = place("x_block", [P, RT, P], F32, offset=chunk_at)
        stats2, _, o = place("stats2", [P, RT, 6], F32, offset=o)
        stats_all, _, o = place("stats_all", [P, NJ, 6], F32, offset=o)
        mean_var2, _, o = place("mean_var2", [P, NJ, 2], F32, offset=o)
        scal2, _, o = place("scal2", [P, 7, NJ], F32, offset=o)
        deg, droot, dinv, var_eps2, std2, row_scale, row_shift = (scal2[:, k, :] for k in range(7))
        assert o <= prob_at

        blk = NJ * BW
        x_in, _, _ = place("x_in", [P, NJ, P], F32, offset=adjT_at + 7 * blk)
        h_in, _, _ = place("h_in", [P, NJ, P], F32, offset=adjT_at + 6 * blk)
        o = adjT_at + 5 * blk
        w_in, _, o = place("w_in", [P, 3, P], F32, offset=o)
        stats, _, o = place("stats", [P, NJ, 6], F32, offset=o)
        mean_var, _, o = place("mean_var", [P, NJ, 2], F32, offset=o)
        var_eps, _, o = place("var_eps", [P, NJ], F32, offset=o)
        std, _, o = place("std", [P, NJ], F32, offset=o)
        rstd, _, o = place("rstd", [P, NJ], F32, offset=o)
        col0, _, o = place("col0", [P, N // P], F32, offset=o)
        col0_set, _, o = place("col0_set", [P, N // P], F32, offset=o)
        col0_sum, _, o = place("col0_sum", [P, 1], F32, offset=o)
        first_row, _, o = place("first_row", [P, NB], I32, offset=o)
        first_row_f, _, o = place("first_row_f", [P, NB], F32, offset=o)
        assert o <= adjT_at + 6 * blk

        o = high_at
        x1, _, o = place("x1", [P, NJ, P], F32, offset=o)
        part, _, o = place("part", [P, 3, NJ, P], BF16, offset=o)
        adj_bf, _, o = place("adj_bf", [P, 2, 2, BW], BF16, offset=o)
        aggT, _, o = place("aggT", [P, BW], F32, offset=o)
        assert o <= chunk_at
        z, _, o = place("z", [P, 2, RT, P], F32, offset=prob_at)
        res, _, o = place("res", [P, 2, RT, P], F32, offset=o)
        assert o <= prob_at + 16 * BW

        def bank(name, shape):
            return ctx.enter_context(nc.psum_tensor(name, shape, F32))

        pS = bank("pS", [P, 2, 2, BW])
        pAcc = bank("pAcc", [P, 2, BW])
        pMisc = bank("pMisc", [P, BW])
        pT = ctx.enter_context(nc.psum_tensor("pT", [P, 4, 2, P], BF16))

        def sem(name):
            return ctx.enter_context(nc.semaphore(name))

        x_loaded, w_loaded, col0_loaded, bias_loaded = sem("x_loaded"), sem("w_loaded"), sem("col0_loaded"), sem("bias_loaded")
        pool_step, consts_ready = sem("pool_step"), sem("consts_ready")
        v_setup, std_ready, h_ready = sem("v_setup"), sem("std_ready"), sem("h_ready")
        ident_ready = sem("ident_ready")
        hT_turned, high_ready, low_ready = sem("hT_turned"), sem("high_ready"), sem("low_ready")
        w_turned, w_high_ready, w_low_ready = sem("w_turned"), sem("w_high_ready"), sem("w_low_ready")
        feat_made, feat_ready, feat_summed, tiny_ready = sem("feat_made"), sem("feat_ready"), sem("feat_summed"), sem("tiny_ready")
        col0_counted, rows_ready, col0_total = sem("col0_counted"), sem("rows_ready"), sem("col0_total")
        chunk_loaded = [sem(f"chunk_loaded{k}") for k in range(PAIRS)]
        chunk_turned, chunk_summed = sem("chunk_turned"), sem("chunk_summed")
        kept_by_act, kept_by_dve = sem("kept_by_act"), sem("kept_by_dve")
        scores_ready = [sem(f"scores_ready{k}") for k in range(2)]
        exp_ready = [sem(f"exp_ready{k}") for k in range(2)]
        prob_ready = [sem(f"prob_ready{k}") for k in range(2)]
        prob_added = [sem(f"prob_added{k}") for k in range(2)]
        half_added = [sem(f"half_added{k}") for k in range(2)]
        prob_used = [sem(f"prob_used{k}") for k in range(2)]
        own_made = [sem(f"own_made{k}") for k in range(2)]
        own_kept = [sem(f"own_kept{k}") for k in range(2)]
        sum_kept = [sem(f"sum_kept{k}") for k in range(2)]
        den_made = [sem(f"den_made{k}") for k in range(2)]
        epi_step = [sem(f"epi_step{k}") for k in range(2)]
        relu_done = [sem(f"relu_done{k}") for k in range(2)]
        stored = sem("stored")
        square_ready, norm_made, norm_read = sem("square_ready"), sem("norm_made"), sem("norm_read")
        h1_loaded = sem("h1_loaded")
        range_known, largest_known = sem("range_known"), sem("largest_known")
        scan_scores, masked, row_max_step = sem("scan_scores"), sem("masked"), sem("row_max_step")
        max_spread, shifted = sem("max_spread"), sem("shifted")
        wg_kept, x_loaded2, x1_stored = sem("wg_kept"), sem("x_loaded2"), sem("x1_stored")
        turned_back, x1_made, stats_made = sem("turned_back"), sem("x1_made"), sem("stats_made")
        stats_kept, mean_var_kept = sem("stats_kept"), sem("mean_var_kept")
        deg_step, deg_ready, deg_rooted = sem("deg_step"), sem("deg_ready"), sem("deg_rooted")
        var2_ready, std2_ready, scale_step, scale_ready = sem("var2_ready"), sem("std2_ready"), sem("scale_step"), sem("scale_ready")
        x1_loaded = [sem(f"x1_loaded{k}") for k in range(NB)]
        z_made, part0_ready, rest_made, part1_ready, part2_ready = (
            sem("z_made"), sem("part0_ready"), sem("rest_made"), sem("part1_ready"), sem("part2_ready"))
        x1_biased = sem("x1_biased")
        adj_wide, adj_used, agg_kept = sem("adj_wide"), sem("adj_used"), sem("agg_kept")
        res_made, res_ready = sem("res_made"), sem("res_ready")
        res_stored = [sem(f"res_stored{k}") for k in range(2)]

        def is_int(v):
            return isinstance(v, int)

        def wait(eng, s, value):
            if is_int(value):
                if value > 0:
                    eng.wait_ge(s, value)
            else:
                eng.wait_ge(s, value)

        def over_blocks(eng, body):
            body(0, 0, False, True)
            body(1, 1, True, True)
            with eng.Fori(1, NB // 2 - 1) as turn:
                body(turn * 2, 0, True, True)
                body(turn * 2 + 1, 1, True, True)
            body(NB - 2, 0, True, True)
            body(NB - 1, 1, True, False)

        def turned_unit(b, u, has_next):
            if u + AHEAD < UNITS:
                return b, u + AHEAD
            return (b + 1, u + AHEAD - UNITS) if has_next else None

        def one_by_one(eng, body):
            body(0, True)
            with eng.Fori(1, NB - 1) as b:
                body(b, True)
            body(NB - 1, False)

        def second_attention(eng, plain, guarded):
            eng.wait_ge(range_known, 1)
            safe = eng.value_load(all_safe[0:1, 0:1], min_val=0, max_val=1)
            with eng.If(safe == 1):
                plain()
            with eng.Else():
                guarded()
            eng.end_ifs()

        def kept_place(b, u):
            q, it = u // 2, 2 * (u % 2)
            if is_int(b):
                return adjT[:, b, 4 * q:4 * q + 4, it * P:(it + 2) * P]
            return adjT[:, bass.ds(b, 1), 4 * q:4 * q + 4, it * P:(it + 2) * P].rearrange("p a t i -> p (a t) i")

        turned = pT[:, :, :, :].rearrange("p t c i -> p t (c i)")

        def adj_unit(b, u):
            if is_int(b):
                return adjT[:, b, 2 * u:2 * u + 2, :]
            return adjT[:, bass.ds(b, 1), 2 * u:2 * u + 2, :].rearrange("p a t i -> p (a t) i")

        def over_pairs(eng, body):
            for par in range(2):
                body(par, par)
            with eng.Fori(1, NB // 2) as turn:
                for par in range(2):
                    body(turn * 2 + par, par)

        BATCH = ((0, (NB - 1) * RT), ((NB - 1) * RT, NB * RT))
        ctx.enter_context(nc.allow_non_contiguous_dma(reason="one column of adj"))
        block = ctx.enter_context(nc.Block())

        @block.sync
        def _(sp):
            def load_unit(b, u):
                q, it = u // 2, 2 * (u % 2)
                if u >= PAIRS or not is_int(b):
                    wait(sp, chunk_turned, b * UNITS + u - PAIRS + 1)
                    wait(sp, chunk_summed, b * UNITS + u - PAIRS + 1)
                rows = adj[bass.ds(b * BW + it * P, 2 * P), q * CW:(q + 1) * CW]
                sp.dma_start(chunk[:, u % PAIRS, :, :], rows.rearrange("(c p) j -> p c j", p=P))\
                    .then_inc(chunk_loaded[u % PAIRS], 16)

            for u in range(UNITS):
                load_unit(0, u)
            with sp.Fori(1, NB) as b:
                for u in range(UNITS):
                    load_unit(b, u)
            sp.wait_ge(stored, 16 * NB)
            sp.wait_ge(prob_used[0], NB * UNITS)
            sp.dma_start(feat[:, :, :].rearrange("p t j -> p (t j)"), h1T_dram[:, :]).then_inc(h1_loaded, 16)
            sp.wait_ge(chunk_turned, NB * UNITS)
            sp.wait_ge(chunk_summed, NB * UNITS)

            def load_x(b):
                wait(sp, x1_stored, b * 16)
                wait(sp, stats_made, b)
                sp.dma_start(x_block[:, :, :], x[bass.ds(b * BW, BW), :].rearrange("(t p) d -> p t d", p=P))\
                    .then_inc(x_loaded2, 16)

            def store_x1(b):
                sp.wait_ge(x1_made, b + 1)
                sp.dma_start(x1_dram[bass.ds(b * BW, BW), :].rearrange("(t p) d -> p t d", p=P), x_block[:, :, :])\
                    .then_inc(x1_stored, 16)

            def load_x1(b):
                sp.dma_start(x1[:, RT * b:RT * (b + 1), :],
                             x1_dram[b * BW:(b + 1) * BW, :].rearrange("(t p) d -> p t d", p=P))\
                    .then_inc(x1_loaded[b], 16)

            load_x(0)
            store_x1(0)
            with sp.Fori(1, NB - 1) as b:
                load_x(b)
                store_x1(b)
            load_x(NB - 1)
            sp.wait_ge(own_made[1], NB)
            sp.wait_ge(prob_used[1], NB * UNITS)
            for b in range(NB - 1):
                load_x1(b)
            store_x1(NB - 1)
            sp.wait_ge(x1_stored, 16 * NB)
            load_x1(NB - 1)
            for k in range(2):
                sp.wait_ge(res_stored[k], 16 * (NB // 2))

        @block.gpsimd
        def _(pool):
            nc.gpsimd.memset(ident[:, :], 0.0).then_inc(pool_step, 1)
            nc.gpsimd.memset(ones[:, :], 1.0).then_inc(consts_ready, 1)
            nc.gpsimd.iota(row_in_block[:, :], pattern=[[1, BW]], base=0, channel_multiplier=0).then_inc(consts_ready, 1)
            nc.gpsimd.iota(first_row[:, :], pattern=[[BW, NB]], base=0, channel_multiplier=0).then_inc(consts_ready, 1)
            pool.wait_ge(pool_step, 1)
            nc.gpsimd.affine_select(out=ident[:, :], in_=ident[:, :], compare_op=ALU.not_equal, fill=1.0, base=0,
                                    pattern=[[-1, P]], channel_multiplier=1).then_inc(consts_ready, 1)
            pool.dma_start(col0[:, :], adj[:, 0:1].rearrange("(p t) a -> p (t a)", p=P)).then_inc(col0_loaded, 16)

            def guarded():
                for b in range(NB):
                    wait(pool, shifted, b * UNITS)
                    wait(pool, epi_step[1], b * EPI)
                    pool.wait_ge(row_max_step, (b + 1) * UNITS * 2)
                    nc.gpsimd.partition_all_reduce(max_all[:, :], row_max[:, :], P, bass.bass_isa.ReduceOp.max)\
                        .then_inc(max_spread, 1)
            second_attention(pool, lambda: None, guarded)
            for b in range(NB):
                rows = x1[:, RT * b:RT * (b + 1), :]
                pool.wait_ge(z_made, b + 1)
                nc.gpsimd.tensor_tensor(rows, rows, bg_all[:, :].rearrange("p (a d) -> p a d", a=1).broadcast_to([P, RT, P]),
                                        ALU.add).then_inc(x1_biased, 1)

        @block.scalar
        def _(act):
            act.dma_start(x_in[:, :, :], x.rearrange("(t p) d -> p t d", p=P)).then_inc(x_loaded, 16)
            for k, w in enumerate((W0, W1, Wg)):
                act.dma_start(w_in[:, k, :], w).then_inc(w_loaded, 16)
            for k, b in enumerate((b0, b1)):
                act.dma_start(bias_col[:, k:k + 1], b.rearrange("(d a) -> d a", a=1)).then_inc(bias_loaded, 16)
            act.dma_start(bg_all[:, :], bg.rearrange("(a d) -> a d", a=1).broadcast_to([P, P])).then_inc(bias_loaded, 16)

            def keep_unit(b, u):
                act.wait_ge(chunk_turned, b * UNITS + u + 1)
                nc.scalar.activation(kept_place(b, u), turned, ACT.Copy).then_inc(kept_by_act, 1)

            def sum_unit(b, u):
                act.wait_ge(chunk_loaded[u % PAIRS], 16 * (b * (UNITS // PAIRS) + u // PAIRS + 1))
                wait(act, chunk_summed, b * UNITS + u)
                for c in range(2):
                    last = nc.scalar.activation(junk[:, c, :], chunk[:, u % PAIRS, c, :], ACT.Copy,
                                                accum_out=deg_part[:, bass.ds(b * CHUNKS + 2 * u + c, 1)])
                last.then_inc(chunk_summed, 1)

            def feat_copies(L):
                for grp in range(NJ // 4):
                    act.wait_ge(feat_made, L * (NJ // 4) + grp + 1)
                    nc.scalar.activation(feat[:, 4 * grp:4 * grp + 4, :],
                                         pS[:, (grp // 2) % 2, grp % 2, :].rearrange("p (t d) -> p t d", t=4),
                                         ACT.Copy).then_inc(feat_ready, 1)

            sum_unit(0, 0)
            keep_unit(0, 0)
            sum_unit(0, 1)
            act.wait_ge(v_setup, 1)
            nc.scalar.activation(std[:, :], var_eps[:, :], ACT.Sqrt).then_inc(std_ready, 1)
            for k in range(2):
                act.wait_ge(w_turned, 3)
                nc.scalar.activation(WT_high[:, k, :], pMisc[:, k * P:(k + 1) * P], ACT.Copy).then_inc(w_high_ready, 1)
            nc.scalar.activation(WgT[:, :], pMisc[:, 3 * P:4 * P], ACT.Copy).then_inc(w_high_ready, 1)
            for grp in range(NJ // 4):
                act.wait_ge(hT_turned, grp + 1)
                nc.scalar.activation(high[:, grp * BW:(grp + 1) * BW], pS[:, (grp // 2) % 2, grp % 2, :],
                                     ACT.Relu).then_inc(high_ready, 1)
            feat_copies(0)
            sum_unit(0, 2)
            keep_unit(0, 2)
            sum_unit(0, 3)

            def epi_own(L, b):
                act.wait_ge(own_made[L], b + 1)
                wait(act, epi_step[L], b * EPI)
                nc.scalar.activation(tB[:, :], pMisc[:, :], ACT.Copy).then_inc(own_kept[L], 1)

            def epi_relu(L, b):
                act.wait_ge(epi_step[L], b * EPI + EPI)
                nc.scalar.activation(tC[:, :], tA[:, :], ACT.Relu, bias=bias_col[:, L:L + 1]).then_inc(relu_done[L], 1)
                if L == 0:
                    act.wait_ge(relu_done[L], b + 1)
                    act.dma_start(h1T_dram[:, bass.ds(b * BW, BW)], tC[:, :]).then_inc(stored, 16)
                    nc.scalar.activation(tA[:, :], tC[:, :], ACT.Square).then_inc(square_ready, 1)

            def attention(L):
                def body(b, par, has_prev, has_next):
                    for u in range(UNITS):
                        g = b * UNITS + u
                        act.wait_ge(scores_ready[L], g + 1)
                        if not (is_int(b) and b == 0 and u < 2):
                            wait(act, prob_used[L], g - 1)
                            wait(act, prob_added[L], g - 1)
                        nc.scalar.activation(prob[:, u % 2, :, :], pS[:, u % 2, :, :], ACT.Exp,
                                             scale=SCALE).then_inc(exp_ready[L], 1)
                        ahead = turned_unit(b, u, has_next)
                        if L == 0 and ahead:
                            if u % 2 == 0:
                                keep_unit(*ahead)
                            sum_unit(*ahead)
                        if has_prev and u == 1:
                            epi_own(L, b - 1)
                        if has_prev and u == 9:
                            epi_relu(L, b - 1)
                        if not has_next and u == UNITS - 1:
                            epi_own(L, b)
                over_blocks(act, body)

            act.wait_ge(bias_loaded, 48)
            attention(0)
            epi_relu(0, NB - 1)
            act.wait_ge(h1_loaded, 16)
            for grp in range(NJ // 4):
                nc.scalar.activation(high[:, grp * BW:(grp + 1) * BW],
                                     feat[:, 4 * grp:4 * grp + 4, :].rearrange("p t j -> p (t j)"),
                                     ACT.Copy).then_inc(high_ready, 1)
            act.wait_ge(low_ready, 2 * (NJ // 4))
            feat_copies(1)

            def guarded():
                def body(b, has_next):
                    for u in range(UNITS):
                        act.wait_ge(shifted, b * UNITS + u + 1)
                        nc.scalar.activation(prob[:, u % 2, :, :], prob[:, u % 2, :, :], ACT.Exp,
                                             scale=SCALE).then_inc(exp_ready[1], 1)
                    epi_own(1, b)
                    if has_next:
                        epi_relu(1, b)
                one_by_one(act, body)
            act.wait_ge(deg_ready, 1)
            nc.scalar.activation(droot, deg, ACT.Sqrt).then_inc(deg_rooted, 1)
            second_attention(act, lambda: attention(1), guarded)

            def roots(batch):
                lo, hi = BATCH[batch]
                act.wait_ge(var2_ready, batch + 1)
                nc.scalar.activation(std2[:, lo:hi], var_eps2[:, lo:hi], ACT.Sqrt).then_inc(std2_ready, 1)

            def first_part(grp):
                act.wait_ge(x1_loaded[grp], 16)
                act.wait_ge(scale_ready, 1 if grp < NB - 1 else 2)
                if grp >= 2:
                    act.wait_ge(part2_ready, grp - 1)
                for t in range(RT):
                    col = RT * grp + t
                    last = nc.scalar.activation(z[:, grp % 2, t, :], x1[:, col, :], ACT.Relu,
                                                bias=row_shift[:, col:col + 1], scale=row_scale[:, col:col + 1])
                last.then_inc(z_made, 1)
                act.wait_ge(z_made, grp + 1)
                nc.scalar.activation(part[:, 0, RT * grp:RT * (grp + 1), :], z[:, grp % 2, :, :], ACT.Copy)\
                    .then_inc(part0_ready, 1)

            def second_part(grp):
                act.wait_ge(rest_made, grp + 1)
                nc.scalar.activation(part[:, 1, RT * grp:RT * (grp + 1), :], z[:, grp % 2, :, :], ACT.Copy)\
                    .then_inc(part1_ready, 1)

            roots(0)
            act.wait_ge(own_made[1], NB)
            act.wait_ge(prob_used[1], NB * UNITS)
            act.wait_ge(sum_kept[1], NB)
            first_part(0)
            epi_relu(1, NB - 1)
            first_part(1)
            second_part(0)
            roots(1)
            for grp in range(2, NB):
                first_part(grp)
                second_part(grp - 1)
            second_part(NB - 1)

            def body(b, par):
                act.wait_ge(adj_used, (b + 1) * UNITS)
                wait(act, res_made, b)
                nc.scalar.activation(aggT[:, :], pAcc[:, par, :], ACT.Copy).then_inc(agg_kept, 1)
                act.wait_ge(res_ready, b + 1)
                act.dma_start(out[bass.ds(b * BW, BW), :].rearrange("(t p) d -> p t d", p=P),
                              res[:, par, :, :]).then_inc(res_stored[par], 16)
            over_pairs(act, body)

        @block.vector
        def _(dve):
            def keep_unit(b, u):
                dve.wait_ge(chunk_turned, b * UNITS + u + 1)
                nc.vector.tensor_copy(kept_place(b, u), turned).then_inc(kept_by_dve, 1)

            dve.wait_ge(consts_ready, 4)
            nc.vector.tensor_copy(ident_bf[:, :], ident[:, :]).then_inc(ident_ready, 1)
            dve.wait_ge(x_loaded, 16)
            for t in range(NJ):
                nc.vector.bn_stats(stats[:, t, :], x_in[:, t, :]).then_inc(h_ready, 1)
            for t in range(NJ):
                dve.wait_ge(h_ready, t + 1)
                nc.vector.bn_aggr(mean_var[:, t, :], stats[:, t, :]).then_inc(h_ready, 1)
            dve.wait_ge(h_ready, 2 * NJ)
            nc.vector.tensor_scalar(var_eps[:, :], mean_var[:, :, 1], EPS_LN, None, ALU.add).then_inc(v_setup, 1)
            dve.wait_ge(std_ready, 1)
            nc.vector.reciprocal(rstd[:, :], std[:, :]).then_inc(v_setup, 1)
            dve.wait_ge(v_setup, 2)
            for t in range(NJ):
                nc.vector.tensor_scalar(h_in[:, t, :], x_in[:, t, :], mean_var[:, t, 0:1], rstd[:, t:t + 1],
                                        ALU.subtract, ALU.mult).then_inc(h_ready, 1)
            keep_unit(0, 1)
            for k in range(2):
                dve.wait_ge(w_high_ready, 3)
                nc.vector.tensor_tensor(WT_low[:, k, :], pMisc[:, k * P:(k + 1) * P],
                                        WT_high[:, k, :].bitcast(F32), ALU.subtract).then_inc(w_low_ready, 1)
            for grp in range(NJ // 4):
                cols = slice(grp * BW, (grp + 1) * BW)
                dve.wait_ge(high_ready, grp + 1)
                nc.vector.scalar_tensor_tensor(out=low[:, cols], in0=pS[:, (grp // 2) % 2, grp % 2, :], scalar=0.0,
                                               in1=high[:, cols].bitcast(F32), op0=ALU.max,
                                               op1=ALU.subtract).then_inc(low_ready, 1)
            dve.wait_ge(col0_loaded, 16)
            nc.vector.tensor_scalar(col0_set[:, :], col0[:, :], 0.0, None, ALU.not_equal).then_inc(v_setup, 1)
            dve.wait_ge(v_setup, 3)
            nc.vector.tensor_reduce(col0_sum[:, :], col0_set[:, :], AX_X, ALU.add).then_inc(col0_counted, 1)
            dve.wait_ge(consts_ready, 4)
            nc.vector.tensor_copy(first_row_f[:, :], first_row[:, :]).then_inc(v_setup, 1)
            dve.wait_ge(v_setup, 4)
            dve.wait_ge(col0_total, 1)
            nc.vector.tensor_scalar(left_in_block[:, :], first_row_f[:, :], -1.0, pMisc[:, 2 * P:2 * P + 1],
                                    ALU.mult, ALU.add).then_inc(rows_ready, 1)
            dve.wait_ge(feat_summed, 1)
            nc.vector.tensor_scalar(tiny_sum[:, 0:1], pMisc[:, 2 * P + 2:2 * P + 3], TINY, None,
                                    ALU.mult).then_inc(tiny_ready, 1)
            dve.wait_ge(tiny_ready, 1)
            dve.wait_ge(rows_ready, 1)
            keep_unit(0, 3)

            def epilogue(L, b, par, step):
                s = epi_step[L]
                if step == 0:
                    dve.wait_ge(den_made[L], b + 1)
                    if L == 0:
                        wait(dve, stored, b * 16)
                        wait(dve, square_ready, b)
                    else:
                        wait(dve, turned_back, b)
                    nc.vector.reciprocal(tC[:, :], pMisc[:, :]).then_inc(s, 1)
                elif step == 1:
                    dve.wait_ge(s, b * EPI + 1)
                    dve.wait_ge(prob_used[L], b * UNITS + UNITS)
                    nc.vector.scalar_tensor_tensor(out=tA[:, :], in0=pAcc[:, par, :], scalar=tiny_sum[:, L:L + 1],
                                                   in1=tC[:, :], op0=ALU.add, op1=ALU.mult).then_inc(s, 1)
                elif step == 2:
                    dve.wait_ge(s, b * EPI + 2)
                    dve.wait_ge(own_kept[L], b + 1)
                    nc.vector.tensor_tensor(tA[:, :], tA[:, :], tB[:, :], ALU.subtract).then_inc(s, 1)
                elif step == 3:
                    dve.wait_ge(s, b * EPI + 3)
                    left = left_in_block[:, b:b + 1] if is_int(b) else left_in_block[:, bass.ds(b, 1)]
                    nc.vector.scalar_tensor_tensor(out=tA[:, :], in0=row_in_block[:, :], scalar=left, in1=tA[:, :],
                                                   op0=ALU.is_ge, op1=ALU.mult).then_inc(s, 1)
                elif step == 4:
                    dve.wait_ge(s, b * EPI + 4)
                    nc.vector.scalar_tensor_tensor(out=tA[:, :], in0=tA[:, :], scalar=0.5, in1=tB[:, :],
                                                   op0=ALU.mult, op1=ALU.add).then_inc(s, 1)

            def epi_norm(b):
                dve.wait_ge(norm_made, b + 1)
                dst = norm_max[:, b:b + 1] if is_int(b) else norm_max[:, bass.ds(b, 1)]
                nc.vector.tensor_reduce(dst, pMisc[:, :], AX_X, ALU.max).then_inc(norm_read, 1)

            def residual(b):
                dve.wait_ge(turned_back, b + 1)
                dve.wait_ge(x_loaded2, 16 * (b + 1))
                nc.vector.tensor_tensor(x_block[:, :, :], x_block[:, :, :],
                                        pMisc[:, :].rearrange("p (t d) -> p t d", t=RT), ALU.add).then_inc(x1_made, 1)

            def statistics(b):
                dve.wait_ge(x1_made, b + 1)
                for t in range(RT):
                    last = nc.vector.bn_stats(stats2[:, t, :], x_block[:, t, :])
                last.then_inc(stats_made, 1)
                dve.wait_ge(stats_made, b + 1)
                nc.vector.tensor_copy(stats_all[:, bass.ds(b * RT, RT), :], stats2[:, :, :]).then_inc(stats_kept, 1)

            def means(blocks):
                dve.wait_ge(stats_kept, blocks[-1] + 1)
                for b in blocks:
                    for t in range(RT * b, RT * (b + 1)):
                        last = nc.vector.bn_aggr(mean_var2[:, t, :], stats_all[:, t, :])
                    last.then_inc(mean_var_kept, 1)

            def attention(L):
                def body(b, par, has_prev, has_next):
                    for u in range(UNITS):
                        if L == 0 and u % 2 == 0:
                            dve.wait_ge(kept_by_act, b * (UNITS // 2) + u // 2 + 1)
                            dve.wait_ge(kept_by_dve, b * (UNITS // 2) + u // 2 + 1)
                        g = b * UNITS + u
                        pr = prob[:, u % 2, :, :]
                        a = adj_unit(b, u)
                        dve.wait_ge(exp_ready[L], g + 1)
                        nc.vector.tensor_tensor(pr, pr, a, ALU.mult).then_inc(prob_ready[L], 1)
                        ahead = turned_unit(b, u, has_next)
                        if L == 0 and ahead and u % 2 == 1:
                            keep_unit(*ahead)
                        add_unit(L, b, u)
                        if has_prev and 4 <= u < 4 + EPI:
                            epilogue(L, b - 1, 1 - par, u - 4)
                        if has_prev and u == 12 and L == 0:
                            epi_norm(b - 1)
                        if has_prev and u == 12 and L == 1:
                            residual(b - 1)
                            statistics(b - 1)
                        if L == 1 and not has_next and u in (2, 3):
                            means(range(3 * u - 6, 3 * u - 3))
                        if L == 1 and not has_next and u == 13:
                            means(range(NB - 2, NB - 1))
                    keep_sum(L, b)

                over_blocks(dve, body)

            def add_unit(L, b, u):
                g = b * UNITS + u
                pr = prob[:, u % 2, :, :]
                dve.wait_ge(prob_ready[L], g + 1)
                if u == 0:
                    wait(dve, sum_kept[L], b)
                    nc.vector.tensor_scalar(psumR[:, :], pr[:, 0, :], (N // P) * TINY, None,
                                            ALU.add).then_inc(half_added[L], 1)
                else:
                    dve.wait_ge(prob_added[L], g)
                    nc.vector.tensor_tensor(psumR[:, :], psumR[:, :], pr[:, 0, :], ALU.add).then_inc(half_added[L], 1)
                dve.wait_ge(half_added[L], g + 1)
                nc.vector.tensor_tensor(psumR[:, :], psumR[:, :], pr[:, 1, :], ALU.add).then_inc(prob_added[L], 1)

            def keep_sum(L, b):
                dve.wait_ge(prob_added[L], b * UNITS + UNITS)
                if L == 0:
                    wait(dve, norm_made, b)
                else:
                    wait(dve, relu_done[L], b)
                nc.vector.tensor_copy(tA[:, :], psumR[:, :]).then_inc(sum_kept[L], 1)

            def guarded():
                def body(b, has_next):
                    if not (is_int(b) and b == 0):
                        dve.wait_ge(relu_done[1], b)
                        dve.wait_ge(prob_used[1], b * UNITS)
                    for u in range(UNITS):
                        g = b * UNITS + u
                        dve.wait_ge(scan_scores, g + 1)
                        wait(dve, row_max_step, 2 * g)
                        nc.vector.tensor_tensor(scan[:, :, :], pS[:, u % 2, :, :], adj_unit(b, u),
                                                ALU.mult).then_inc(masked, 1)
                        dve.wait_ge(masked, g + 1)
                        if u == 0:
                            wait(dve, max_spread, b)
                            nc.vector.tensor_copy(row_max[:, :], scan[:, 0, :]).then_inc(row_max_step, 1)
                        else:
                            nc.vector.tensor_tensor(row_max[:, :], row_max[:, :], scan[:, 0, :],
                                                    ALU.max).then_inc(row_max_step, 1)
                        dve.wait_ge(row_max_step, 2 * g + 1)
                        nc.vector.tensor_tensor(row_max[:, :], row_max[:, :], scan[:, 1, :],
                                                ALU.max).then_inc(row_max_step, 1)
                        dve.wait_ge(row_max_step, 2 * g + 2)
                    dve.wait_ge(max_spread, b + 1)
                    for u in range(UNITS):
                        g = b * UNITS + u
                        pr = prob[:, u % 2, :, :]
                        dve.wait_ge(scores_ready[1], g + 1)
                        if not (is_int(b) and b == 0 and u < 2):
                            dve.wait_ge(prob_used[1], g - 1)
                            dve.wait_ge(prob_added[1], g - 1)
                        for h in range(2):
                            last = nc.vector.tensor_tensor(pr[:, h, :], pS[:, u % 2, h, :], max_all[:, :],
                                                           ALU.subtract)
                        last.then_inc(shifted, 1)
                        dve.wait_ge(exp_ready[1], g + 1)
                        nc.vector.scalar_tensor_tensor(out=pr, in0=pr, scalar=3e38, in1=adj_unit(b, u),
                                                       op0=ALU.min, op1=ALU.mult).then_inc(prob_ready[1], 1)
                        add_unit(1, b, u)
                    keep_sum(1, b)
                    if has_next:
                        for step in range(EPI):
                            epilogue(1, b, 1, step)
                        residual(b)
                        statistics(b)
                    else:
                        means(range(NB - 1))
                one_by_one(dve, body)

            attention(0)
            for step in range(EPI):
                epilogue(0, NB - 1, 1, step)
            epi_norm(NB - 1)
            dve.wait_ge(norm_read, NB)
            nc.vector.tensor_reduce(largest[:, :], norm_max[:, :], AX_X, ALU.max).then_inc(largest_known, 1)
            dve.wait_ge(largest_known, 1)
            nc.vector.tensor_scalar(all_safe[:, :], largest[:, :], SAFE_SCORE / SCALE, None,
                                    ALU.is_le).then_inc(range_known, 1)
            dve.wait_ge(chunk_summed, NB * UNITS)
            dve.wait_ge(chunk_turned, NB * UNITS)
            nc.vector.tensor_reduce(deg.rearrange("p (b t) -> p b t", t=RT),
                                    deg_part[:, :].rearrange("p (b q t) -> p b t q", q=CPR, t=RT), AX_X,
                                    ALU.add).then_inc(deg_step, 1)
            dve.wait_ge(deg_step, 1)
            nc.vector.tensor_scalar(deg, deg, 1.0, None, ALU.add).then_inc(deg_ready, 1)
            dve.wait_ge(h1_loaded, 16)
            for grp in range(NJ // 4):
                cols = slice(grp * BW, (grp + 1) * BW)
                dve.wait_ge(high_ready, NJ // 4 + grp + 1)
                nc.vector.tensor_tensor(low[:, cols], feat[:, 4 * grp:4 * grp + 4, :].rearrange("p t j -> p (t j)"),
                                        high[:, cols].bitcast(F32), ALU.subtract).then_inc(low_ready, 1)
            dve.wait_ge(feat_summed, 2)
            nc.vector.tensor_scalar(tiny_sum[:, 1:2], pMisc[:, 2 * P + 2:2 * P + 3], TINY, None,
                                    ALU.mult).then_inc(tiny_ready, 1)
            dve.wait_ge(tiny_ready, 2)
            second_attention(dve, lambda: attention(1), guarded)

            def variances(batch):
                lo, hi = BATCH[batch]
                dve.wait_ge(mean_var_kept, hi // RT)
                nc.vector.tensor_scalar(var_eps2[:, lo:hi], mean_var2[:, lo:hi, 1], EPS_LN, None,
                                        ALU.add).then_inc(var2_ready, 1)

            def scales(batch):
                lo, hi = BATCH[batch]
                dve.wait_ge(std2_ready, batch + 1)
                dve.wait_ge(deg_rooted, 1)
                if batch == 0:
                    nc.vector.reciprocal(dinv, droot).then_inc(deg_step, 1)
                nc.vector.reciprocal(var_eps2[:, lo:hi], std2[:, lo:hi]).then_inc(scale_step, 1)
                dve.wait_ge(deg_step, 2)
                dve.wait_ge(scale_step, 2 * batch + 1)
                nc.vector.tensor_tensor(row_scale[:, lo:hi], var_eps2[:, lo:hi], dinv[:, lo:hi],
                                        ALU.mult).then_inc(scale_step, 1)
                dve.wait_ge(scale_step, 2 * batch + 2)
                nc.vector.scalar_tensor_tensor(out=row_shift[:, lo:hi], in0=mean_var2[:, lo:hi, 0], scalar=-1.0,
                                               in1=row_scale[:, lo:hi], op0=ALU.mult,
                                               op1=ALU.mult).then_inc(scale_ready, 1)

            def other_parts(grp):
                dve.wait_ge(part0_ready, grp + 1)
                tiles = slice(RT * grp, RT * (grp + 1))
                nc.vector.tensor_tensor(z[:, grp % 2, :, :], z[:, grp % 2, :, :], part[:, 0, tiles, :],
                                        ALU.subtract).then_inc(rest_made, 1)
                dve.wait_ge(part1_ready, grp + 1)
                nc.vector.tensor_tensor(part[:, 2, tiles, :], z[:, grp % 2, :, :], part[:, 1, tiles, :],
                                        ALU.subtract).then_inc(part2_ready, 1)

            variances(0)
            scales(0)
            for step in range(EPI):
                epilogue(1, NB - 1, 1, step)

            def body(b, par):
                for u in range(UNITS):
                    g = b * UNITS + u
                    if is_int(b) and b == 0 and u % 2 == 0:
                        other_parts(u // 2)
                    if not (is_int(b) and b == 0 and u < 2):
                        dve.wait_ge(adj_used, g - 1)
                    nc.vector.tensor_copy(adj_bf[:, u % 2, :, :], adj_unit(b, u)).then_inc(adj_wide, 1)
                    if is_int(b) and b == 0 and u == 1:
                        residual(NB - 1)
                        statistics(NB - 1)
                        means(range(NB - 1, NB))
                        variances(1)
                    if is_int(b) and b == 0 and u == 3:
                        scales(1)
                    if u == 2 and not (is_int(b) and b == 0):
                        finish(b - 1, 1 - par)

            def finish(b, par):
                dve.wait_ge(res_made, b + 1)
                dve.wait_ge(x1_biased, NB)
                if not (is_int(b) and b < 2):
                    dve.wait_ge(res_stored[par], (b - par) * 8)
                for t in range(RT):
                    row = b * RT + t
                    last = nc.vector.scalar_tensor_tensor(
                        out=res[:, par, t, :], in0=pMisc[:, t * P:(t + 1) * P], scalar=scal2[:, 2, bass.ds(row, 1)],
                        in1=x1[:, bass.ds(row, 1), :].rearrange("p a d -> p (a d)"), op0=ALU.mult, op1=ALU.add)
                last.then_inc(res_ready, 1)
            over_pairs(dve, body)
            finish(NB - 1, 1)

        @block.tensor
        def _(pe):
            pe.wait_ge(consts_ready, 4)

            def turn_unit(b, u):
                pe.wait_ge(chunk_loaded[u % PAIRS], 16 * (b * (UNITS // PAIRS) + u // PAIRS + 1))
                if u % 2:
                    pe.wait_ge(kept_by_act, b * (UNITS // 2) + u // 2 + 1)
                else:
                    wait(pe, kept_by_dve, b * (UNITS // 2) + u // 2)
                for c in range(2):
                    upper = chunk[:, u % PAIRS, c, :].bitcast(BF16).rearrange("p (j two) -> p j two", two=2)[:, :, 1]
                    for m in range(4):
                        mm = nc.tensor.transpose(pT[:, m, c, :], upper[:, m * P:(m + 1) * P], ident_bf[:, :])
                mm.then_inc(chunk_turned, 1)

            def product3(dst, a_high, a_low, b_high, b_low):
                nc.tensor.matmul(dst, a_high, b_high, start=True, stop=False)
                nc.tensor.matmul(dst, a_high, b_low, start=False, stop=False)
                return nc.tensor.matmul(dst, a_low, b_high, start=False, stop=True)

            def make_feat(L):
                for grp in range(NJ // 4):
                    pe.wait_ge(low_ready, L * (NJ // 4) + (grp + 1 if L == 0 else NJ // 4))
                    if grp >= 4:
                        pe.wait_ge(feat_ready, L * (NJ // 4) + grp - 3)
                    else:
                        pe.wait_ge(low_ready, L * (NJ // 4) + (grp + 5 if L == 0 else NJ // 4))
                    for t in range(4 * grp, 4 * grp + 4):
                        mm = product3(pS[:, (grp // 2) % 2, grp % 2, (t % 4) * P:(t % 4 + 1) * P],
                                      high[:, t * P:(t + 1) * P], low[:, t * P:(t + 1) * P],
                                      WT_high[:, L, :], WT_low[:, L, :])
                    mm.then_inc(feat_made, 1)
                pe.wait_ge(feat_ready, (L + 1) * (NJ // 4))
                pe.wait_ge(rows_ready, 1)
                for t in range(NJ):
                    mm = nc.tensor.matmul(pMisc[:, 2 * P + 2:2 * P + 3], feat[:, t, :], ones[:, 0:1],
                                          start=(t == 0), stop=(t == NJ - 1))
                mm.then_inc(feat_summed, 1)

            pe.wait_ge(ident_ready, 1)
            turn_unit(0, 0)
            turn_unit(0, 1)
            pe.wait_ge(w_loaded, 48)
            for k, at_col in enumerate((0, P, 3 * P)):
                nc.tensor.transpose(pMisc[:, at_col:at_col + P], w_in[:, k, :], ident[:, :]).then_inc(w_turned, 1)
            for grp in range(NJ // 4):
                pe.wait_ge(h_ready, 2 * NJ + 4 * grp + 4)
                if grp >= 4:
                    pe.wait_ge(low_ready, grp - 3)
                for t in range(4 * grp, 4 * grp + 4):
                    mm = nc.tensor.transpose(pS[:, (grp // 2) % 2, grp % 2, (t % 4) * P:(t % 4 + 1) * P],
                                             h_in[:, t, :], ident[:, :])
                mm.then_inc(hT_turned, 1)
            pe.wait_ge(w_low_ready, 2)
            pe.wait_ge(col0_counted, 1)
            nc.tensor.matmul(pMisc[:, 2 * P:2 * P + 1], ones[:, :], col0_sum[:, :], start=True, stop=True)\
                .then_inc(col0_total, 1)
            make_feat(0)
            turn_unit(0, 2)
            turn_unit(0, 3)

            def unit_scores(b, u):
                rows = bass.ds(b * BW, BW)
                for h in range(2):
                    t = 2 * u + h
                    mm = product3(pS[:, u % 2, h, :], high[:, t * P:(t + 1) * P], low[:, t * P:(t + 1) * P],
                                  high[:, rows], low[:, rows])
                return mm

            def scores(L, b, u):
                if not (is_int(b) and b == 0 and u < 2):
                    pe.wait_ge(exp_ready[L], b * UNITS + u - 1)
                unit_scores(b, u).then_inc(scores_ready[L], 1)

            def own(L, b):
                if L == 0:
                    wait(pe, norm_read, b)
                else:
                    wait(pe, x1_made, b)
                rows = bass.ds(b * BW, BW)
                product3(pMisc[:, :], WT_high[:, L, :], WT_low[:, L, :], high[:, rows], low[:, rows])\
                    .then_inc(own_made[L], 1)

            def denominator(L, b):
                pe.wait_ge(own_kept[L], b + 1)
                pe.wait_ge(sum_kept[L], b + 1)
                nc.tensor.matmul(pMisc[:, :], ones[:, :], tA[:, :], start=True, stop=True).then_inc(den_made[L], 1)

            def norms(b):
                pe.wait_ge(square_ready, b + 1)
                nc.tensor.matmul(pMisc[:, :], ones[:, :], tA[:, :], start=True, stop=True).then_inc(norm_made, 1)

            def turn_back(b):
                pe.wait_ge(relu_done[1], b + 1)
                for t in range(RT):
                    mm = nc.tensor.transpose(pMisc[:, t * P:(t + 1) * P], tC[:, t * P:(t + 1) * P], ident[:, :])
                mm.then_inc(turned_back, 1)

            def mix(L, b, par, u):
                pe.wait_ge(prob_ready[L], b * UNITS + u + 1)
                for h in range(2):
                    mm = nc.tensor.matmul(pAcc[:, par, :], feat[:, 2 * u + h, :], prob[:, u % 2, h, :],
                                          start=(u == 0 and h == 0), stop=(u == UNITS - 1 and h == 1))
                mm.then_inc(prob_used[L], 1)

            def attention(L):
                def body(b, par, has_prev, has_next):
                    for u in range(UNITS):
                        ahead = turned_unit(b, u, has_next)
                        if L == 0 and ahead:
                            turn_unit(*ahead)
                        if u < UNITS - 1:
                            scores(L, b, u + 1)
                        elif has_next:
                            scores(L, b + 1, 0)
                        if has_prev and u == 1:
                            own(L, b - 1)
                        if has_prev and u == 3:
                            denominator(L, b - 1)
                        if has_prev and u == 11:
                            norms(b - 1) if L == 0 else turn_back(b - 1)
                        if not has_next and u == 14:
                            own(L, b)
                        if u == 0 and not (is_int(b) and b < 2):
                            pe.wait_ge(epi_step[L], (b - 1) * EPI)
                        mix(L, b, par, u)

                pe.wait_ge(tiny_ready, L + 1)
                scores(L, 0, 0)
                over_blocks(pe, body)

            def guarded():
                def body(b, has_next):
                    for u in range(UNITS):
                        g = b * UNITS + u
                        if u < 2:
                            wait(pe, shifted, b * UNITS)
                        else:
                            pe.wait_ge(row_max_step, 2 * g - 2)
                        unit_scores(b, u).then_inc(scan_scores, 1)
                    pe.wait_ge(max_spread, b + 1)
                    for u in range(UNITS):
                        if u >= 2:
                            pe.wait_ge(shifted, b * UNITS + u - 1)
                        unit_scores(b, u).then_inc(scores_ready[1], 1)
                        if u >= 1:
                            if u == 1:
                                wait(pe, epi_step[1], b * EPI)
                            mix(1, b, 1, u - 1)
                    mix(1, b, 1, UNITS - 1)
                    own(1, b)
                    if has_next:
                        denominator(1, b)
                        turn_back(b)
                one_by_one(pe, body)

            attention(0)
            denominator(0, NB - 1)
            norms(NB - 1)
            pe.wait_ge(norm_read, NB)
            make_feat(1)
            pe.wait_ge(tiny_ready, 2)
            second_attention(pe, lambda: attention(1), guarded)

            denominator(1, NB - 1)
            turn_back(NB - 1)

            def body(b, par):
                for u in range(UNITS):
                    pe.wait_ge(adj_wide, b * UNITS + u + 1)
                    if is_int(b) and b == 0 and u % 2 == 0:
                        pe.wait_ge(part2_ready, u // 2 + 1)
                    if u == 0 and not (is_int(b) and b < 2):
                        pe.wait_ge(agg_kept, b - 1)
                    if u == UNITS - 1:
                        for t in range(RT):
                            for k in range(3):
                                own = part[:, k, bass.ds(b * RT + t, 1), :].rearrange("p a d -> p (a d)")
                                nc.tensor.matmul(pAcc[:, par, t * P:(t + 1) * P], own, ident_bf[:, :], start=False,
                                                 stop=False, skip_group_check=True)
                    for h in range(2):
                        for k in range(3):
                            mm = nc.tensor.matmul(pAcc[:, par, :], part[:, k, 2 * u + h, :], adj_bf[:, u % 2, h, :],
                                                  start=(u == 0 and h == 0 and k == 0),
                                                  stop=(u == UNITS - 1 and h == 1 and k == 2))
                    mm.then_inc(adj_used, 1)
                    if u == 1 and not (is_int(b) and b == 0):
                        project(b - 1)

            def project(b):
                pe.wait_ge(agg_kept, b + 1)
                wait(pe, res_ready, b)
                pe.wait_ge(x1_made, NB)
                for t in range(RT):
                    mm = nc.tensor.matmul(pMisc[:, t * P:(t + 1) * P], aggT[:, t * P:(t + 1) * P], WgT[:, :],
                                          start=True, stop=True)
                mm.then_inc(res_made, 1)
            over_pairs(pe, body)
            project(NB - 1)


_INS = ['x', 'adj', 'L0_gnn_W0', 'L0_gnn_b0', 'L0_gnn_W1', 'L0_gnn_b1', 'L1_gnn_W', 'L1_gnn_b']
_OUTS = [((4096, 128), 'float32')]


def kernel(**inputs):
    import numpy as _np
    import concourse.bacc as _bacc
    from concourse import mybir as _mybir
    from concourse.bass_utils import run_bass_kernel_spmd as _run

    nc = _bacc.Bacc("TRN2", target_bir_lowering=False, num_devices=1)
    arrays, args = {}, []
    for name in _INS:
        a = _np.ascontiguousarray(inputs[name])
        arrays[f"in_{name}_dram"] = a
        args.append(nc.dram_tensor(f"in_{name}_dram", a.shape, _mybir.dt.from_np(a.dtype), kind="ExternalInput").ap())
    for i, (shape, dtype) in enumerate(_OUTS):
        dt = _mybir.dt.from_np(_np.dtype(dtype))
        args.append(nc.dram_tensor(f"out_{i}_dram", shape, dt, kind="ExternalOutput").ap())
    build(nc, *args)
    r = _run(nc, [arrays], core_ids=[0])
    return r.results[0]["out_0_dram"]
```

```python
from contextlib import ExitStack

import concourse.bass as bass
from concourse import mybir

ALU = mybir.AluOpType
ACT = mybir.ActivationFunctionType
AX_X = mybir.AxisListType.X
F32 = mybir.dt.float32
F32R = mybir.dt.float32r
BF16 = mybir.dt.bfloat16
U8 = mybir.dt.uint8
U16 = mybir.dt.uint16
I32 = mybir.dt.int32

P = 128
EPS_LN = 1e-5
TINY = 2.0 ** -100
SAFE_SCORE = 60.0


def build(nc, x, adj, W0, b0, W1, b1, Wg, bg, out):
    N, E = x.shape
    assert E == P
    BW = 512
    NB = N // BW
    NJ = N // P
    UNITS = NJ // 2
    RT = BW // P
    CW = 512
    CPR = N // CW
    CHUNKS = RT * CPR
    PAIRS = 2
    AHEAD = 4
    SCALE = float(E) ** -0.5
    INV = 4
    EPI = INV + 4
    SLOTS = 4
    assert CHUNKS == 2 * UNITS and UNITS % PAIRS == 0 and NB % 2 == 0

    h1T_dram = nc.dram_tensor("h1T_scratch", [P, N], F32, kind="Internal").ap()
    x1_dram = nc.dram_tensor("x1_scratch", [N, E], F32, kind="Internal").ap()

    with ExitStack() as ctx:
        base = -(-nc.sbuf_base // 32) * 32
        at = {"next": base}
        SIZE = {F32: 4, F32R: 4, BF16: 2, U8: 1, U16: 2, I32: 4}

        def place(name, shape, dt, offset=None):
            n = SIZE[dt]
            for s in shape[1:]:
                n *= s
            n = -(-n // 32) * 32
            if offset is None:
                offset = at["next"]
                at["next"] += n
            return nc.alloc_sbuf_tensor_at(name, list(shape), dt, offset=offset), offset, offset + n

        adjT, adjT_at, _ = place("adjT", [P, NB, NJ, BW], U8)
        high, high_at, _ = place("high", [P, N], F32R)
        low, _, _ = place("low", [P, N], F32R)
        feat, _, _ = place("feat", [P, NJ, P], F32)
        chunk, chunk_at, _ = place("chunk", [P, PAIRS, 2, CW], F32)
        prob, prob_at, _ = place("prob", [P, 2, 2, BW], F32)
        psumR, _, _ = place("prob_sum", [P, BW], F32)
        tA, _, _ = place("tA", [P, BW], F32)
        tB, _, _ = place("tB", [P, BW], F32)
        tC, _, _ = place("tC", [P, BW], F32)
        ident, _, _ = place("ident", [P, P], F32)
        ident_bf, _, _ = place("ident_bf", [P, P], BF16)
        WT_high, _, _ = place("WT_high", [P, 2, P], F32R)
        WT_low, _, _ = place("WT_low", [P, 2, P], F32R)
        row_in_block, _, _ = place("row_in_block", [P, BW], U16)
        junk, junk_at, _ = place("junk", [P, 2, CW], U8)
        deg_part, _, _ = place("deg_part", [P, NB * CHUNKS], F32)
        bias_col, _, _ = place("bias_col", [P, 2], F32)
        tiny_sum, _, _ = place("tiny_sum", [P, 2], F32)
        left_in_block, _, _ = place("left_in_block", [P, NB], F32)
        norm_max, _, _ = place("norm_max", [P, NB], F32)
        all_safe, _, _ = place("all_safe", [P, 1], I32)
        largest, _, _ = place("largest", [P, 1], F32)
        WgT, _, _ = place("WgT", [P, P], F32)
        bg_all, _, _ = place("bg_all", [P, P], F32)
        ones, _, work_end = place("ones", [P, P], F32)
        assert work_end <= nc.sbuf_usable_end, work_end - nc.sbuf_usable_end

        scan = prob[:, 0, :, :]
        row_max, max_all = tA, tB
        feat_total = tB[:, :].rearrange("p (t d) -> p t d", t=4)

        diag_plus, _, _ = place("diag_plus", [P, RT, P], BF16, offset=junk_at)

        x_block, _, o = place("x_block", [P, RT, P], F32, offset=chunk_at)
        stats2, _, o = place("stats2", [P, RT, 6], F32, offset=o)
        stats_all, _, o = place("stats_all", [P, NJ, 6], F32, offset=o)
        mean_var2, _, o = place("mean_var2", [P, NJ, 2], F32, offset=o)
        scal2, _, o = place("scal2", [P, 7, NJ], F32, offset=o)
        deg, droot, dinv, var_eps2, std2, row_scale, row_shift = (scal2[:, k, :] for k in range(7))
        res, _, o = place("res", [P, 2, RT, P], F32, offset=o)
        assert o <= prob_at
        z = res

        blk = NJ * BW
        x_in, _, _ = place("x_in", [P, NJ, P], F32, offset=adjT_at + 7 * blk)
        h_in, _, _ = place("h_in", [P, NJ, P], F32, offset=adjT_at + 6 * blk)
        o = adjT_at + 5 * blk
        w_in, _, o = place("w_in", [P, 3, P], F32, offset=o)
        stats, _, o = place("stats", [P, NJ, 6], F32, offset=o)
        mean_var, _, o = place("mean_var", [P, NJ, 2], F32, offset=o)
        var_eps, _, o = place("var_eps", [P, NJ], F32, offset=o)
        std, _, o = place("std", [P, NJ], F32, offset=o)
        rstd, _, o = place("rstd", [P, NJ], F32, offset=o)
        col0, _, o = place("col0", [P, N // P], F32, offset=o)
        col0_set, _, o = place("col0_set", [P, N // P], F32, offset=o)
        col0_sum, _, o = place("col0_sum", [P, 1], F32, offset=o)
        first_row, _, o = place("first_row", [P, NB], I32, offset=o)
        first_row_f, _, o = place("first_row_f", [P, NB], F32, offset=o)
        assert o <= adjT_at + 6 * blk

        o = high_at
        x1, _, o = place("x1", [P, NJ, P], F32, offset=o)
        z_high, _, o = place("z_high", [P, NJ, P], F32R, offset=o)
        z_low, _, o = place("z_low", [P, NJ, P], F32R, offset=o)
        assert o <= chunk_at
        adj_wide, _, o = place("adj_wide", [P, SLOTS, BW], F32R, offset=prob_at)
        assert o <= prob_at + 16 * BW
        aggT = psumR

        def bank(name, shape):
            return ctx.enter_context(nc.psum_tensor(name, shape, F32))

        pS = bank("pS", [P, 2, 2, BW])
        pAcc = bank("pAcc", [P, 2, BW])
        pMisc = bank("pMisc", [P, BW])
        pT = ctx.enter_context(nc.psum_tensor("pT", [P, 4, 2, P], BF16))

        def sem(name):
            return ctx.enter_context(nc.semaphore(name))

        x_loaded = [sem(f"x_part_loaded{k}") for k in range(4)]
        w_loaded, col0_loaded, bias_loaded = sem("w_loaded"), sem("col0_loaded"), sem("bias_loaded")
        pool_step, consts_ready = sem("pool_step"), sem("consts_ready")
        var_ready, std_ready, rstd_ready, h_ready = sem("var_ready"), sem("std_ready"), sem("rstd_ready"), sem("h_ready")
        x_stats, x_means, col0_step = sem("x_stats"), sem("x_means"), sem("col0_step")
        ident_ready = sem("ident_ready")
        hT_turned, high_ready, low_ready = sem("hT_turned"), sem("high_ready"), sem("low_ready")
        w_turned, w_high_ready, w_low_ready = sem("w_turned"), sem("w_high_ready"), sem("w_low_ready")
        feat_made, feat_ready, feat_summed, tiny_ready = sem("feat_made"), sem("feat_ready"), sem("feat_summed"), sem("tiny_ready")
        feat_totalled = sem("feat_totalled")
        col0_counted, rows_ready, col0_total = sem("col0_counted"), sem("rows_ready"), sem("col0_total")
        chunk_loaded = [sem(f"chunk_loaded{k}") for k in range(PAIRS)]
        chunk_turned, chunk_summed = sem("chunk_turned"), sem("chunk_summed")
        kept_by_act, kept_by_dve = sem("kept_by_act"), sem("kept_by_dve")
        scores_ready = [sem(f"scores_ready{k}") for k in range(2)]
        exp_ready = [sem(f"exp_ready{k}") for k in range(2)]
        prob_ready = [sem(f"prob_ready{k}") for k in range(2)]
        prob_added = [sem(f"prob_added{k}") for k in range(2)]
        half_added = [sem(f"half_added{k}") for k in range(2)]
        prob_used = [sem(f"prob_used{k}") for k in range(2)]
        own_made = [sem(f"own_made{k}") for k in range(2)]
        own_kept = [sem(f"own_kept{k}") for k in range(2)]
        sum_kept = [sem(f"sum_kept{k}") for k in range(2)]
        den_made = [sem(f"den_made{k}") for k in range(2)]
        epi_step = [sem(f"epi_step{k}") for k in range(2)]
        relu_done = [sem(f"relu_done{k}") for k in range(2)]
        stored = sem("stored")
        square_ready, norm_made, norm_read = sem("square_ready"), sem("norm_made"), sem("norm_read")
        h1_loaded = [sem(f"h1_loaded{k}") for k in range(4)]
        range_known, largest_known = sem("range_known"), sem("largest_known")
        scan_scores, masked, row_max_step = sem("scan_scores"), sem("masked"), sem("row_max_step")
        max_spread, shifted = sem("max_spread"), sem("shifted")
        x_block_loaded, x1_stored = sem("x_block_loaded"), sem("x1_stored")
        turned_back, x1_made, stats_made = sem("turned_back"), sem("x1_made"), sem("stats_made")
        stats_kept, mean_var_kept = sem("stats_kept"), sem("mean_var_kept")
        deg_step, deg_ready = sem("deg_step"), sem("deg_ready")
        var2_ready, std2_ready, scale_step, scale_ready = sem("var2_ready"), sem("std2_ready"), sem("scale_step"), sem("scale_ready")
        x1_loaded = [sem(f"x1_loaded{k}") for k in range(NB)]
        z_made, z_high_ready, z_low_ready = sem("z_made"), sem("z_high_ready"), sem("z_low_ready")
        x1_biased = sem("x1_biased")
        wide_by_dve, wide_by_act = sem("wide_by_dve"), sem("wide_by_act")
        diag_step, self_loops = sem("diag_step"), sem("self_loops")
        adj_used, agg_kept = sem("adj_used"), sem("agg_kept")
        res_made, res_ready = sem("res_made"), sem("res_ready")
        res_stored = [sem(f"res_stored{k}") for k in range(2)]

        def is_int(v):
            return isinstance(v, int)

        def wait(eng, s, value):
            if is_int(value):
                if value > 0:
                    eng.wait_ge(s, value)
            else:
                eng.wait_ge(s, value)

        def over_blocks(eng, body):
            body(0, 0, False, True)
            body(1, 1, True, True)
            with eng.Fori(1, NB // 2 - 1) as turn:
                body(turn * 2, 0, True, True)
                body(turn * 2 + 1, 1, True, True)
            body(NB - 2, 0, True, True)
            body(NB - 1, 1, True, False)

        def turned_unit(b, u, has_next):
            if u + AHEAD < UNITS:
                return b, u + AHEAD
            return (b + 1, u + AHEAD - UNITS) if has_next else None

        def one_by_one(eng, body):
            body(0, True)
            with eng.Fori(1, NB - 1) as b:
                body(b, True)
            body(NB - 1, False)

        def second_attention(eng, plain, guarded):
            eng.wait_ge(range_known, 1)
            safe = eng.value_load(all_safe[0:1, 0:1], min_val=0, max_val=1)
            with eng.If(safe == 1):
                plain()
            with eng.Else():
                guarded()
            eng.end_ifs()

        def kept_by_vector(u):
            return u % 4 == 3

        def kept_before(b, u):
            return b * (3 * UNITS // 4) + 3 * (u // 4) + u % 4, b * (UNITS // 4) + u // 4

        def kept_place(b, u):
            q, it = u // 2, 2 * (u % 2)
            if is_int(b):
                return adjT[:, b, 4 * q:4 * q + 4, it * P:(it + 2) * P]
            return adjT[:, bass.ds(b, 1), 4 * q:4 * q + 4, it * P:(it + 2) * P].rearrange("p a t i -> p (a t) i")

        turned = pT[:, :, :, :].rearrange("p t c i -> p t (c i)")

        def adj_unit(b, u):
            if is_int(b):
                return adjT[:, b, 2 * u:2 * u + 2, :]
            return adjT[:, bass.ds(b, 1), 2 * u:2 * u + 2, :].rearrange("p a t i -> p (a t) i")

        def adj_tile(b, t):
            if is_int(b):
                return adjT[:, b, t, :]
            return adjT[:, bass.ds(b, 1), t, :].rearrange("p a i -> p (a i)")

        def widened_by_act(b, t):
            return t % 2 == 1 and not (is_int(b) and b == 0)

        def widened_before(b, t):
            if is_int(b) and b == 0:
                return 0, t
            return b * (NJ // 2) - NJ // 2 + t // 2, b * (NJ // 2) + NJ // 2 + (t + 1) // 2

        def over_pairs(eng, body):
            for par in range(2):
                body(par, par)
            with eng.Fori(1, NB // 2) as turn:
                for par in range(2):
                    body(turn * 2 + par, par)

        GROUPS = NJ // 4
        LN = 4
        LT = NJ // LN

        def group_bank(grp):
            return pS[:, (grp // 2) % 2, grp % 2, :]

        def feat_bank(L, grp):
            return pAcc[:, grp % 2, :] if L == 0 else group_bank(grp)

        PROJECT, FINISH = 7, 12
        BATCH = ((0, (NB - 1) * RT), ((NB - 1) * RT, NB * RT))
        ctx.enter_context(nc.allow_non_contiguous_dma(reason="one column of adj"))
        block = ctx.enter_context(nc.Block())

        @block.sync
        def _(sp):
            def load_unit(b, u):
                q, it = u // 2, 2 * (u % 2)
                if u >= PAIRS or not is_int(b):
                    wait(sp, chunk_turned, b * UNITS + u - PAIRS + 1)
                    wait(sp, chunk_summed, b * UNITS + u - PAIRS + 1)
                rows = adj[bass.ds(b * BW + it * P, 2 * P), q * CW:(q + 1) * CW]
                sp.dma_start(chunk[:, u % PAIRS, :, :], rows.rearrange("(c p) j -> p c j", p=P))\
                    .then_inc(chunk_loaded[u % PAIRS], 16)

            for u in range(UNITS):
                load_unit(0, u)
            with sp.Fori(1, NB) as b:
                for u in range(UNITS):
                    load_unit(b, u)
            sp.wait_ge(chunk_turned, NB * UNITS)
            sp.wait_ge(chunk_summed, NB * UNITS)
            for grp in range(GROUPS - 1):
                sp.wait_ge(stored, 16 * (grp + 1))
                if grp >= 4:
                    sp.wait_ge(low_ready, GROUPS + grp - 3)
                sp.dma_start(chunk[:, (grp // 2) % 2, grp % 2, :], h1T_dram[:, grp * BW:(grp + 1) * BW])\
                    .then_inc(h1_loaded[grp % 4], 16)
            sp.wait_ge(low_ready, 2 * GROUPS)

            def load_x(b):
                wait(sp, x1_stored, b * 16)
                wait(sp, stats_made, b)
                sp.dma_start(x_block[:, :, :], x[bass.ds(b * BW, BW), :].rearrange("(t p) d -> p t d", p=P))\
                    .then_inc(x_block_loaded, 16)

            def store_x1(b):
                sp.wait_ge(x1_made, b + 1)
                sp.dma_start(x1_dram[bass.ds(b * BW, BW), :].rearrange("(t p) d -> p t d", p=P), x_block[:, :, :])\
                    .then_inc(x1_stored, 16)

            def load_x1(b):
                sp.dma_start(x1[:, RT * b:RT * (b + 1), :],
                             x1_dram[b * BW:(b + 1) * BW, :].rearrange("(t p) d -> p t d", p=P))\
                    .then_inc(x1_loaded[b], 16)

            load_x(0)
            store_x1(0)
            with sp.Fori(1, NB - 1) as b:
                load_x(b)
                store_x1(b)
            load_x(NB - 1)
            sp.wait_ge(own_made[1], NB)
            sp.wait_ge(scores_ready[1], NB * UNITS)
            for b in range(NB - 1):
                load_x1(b)
            store_x1(NB - 1)
            sp.wait_ge(x1_stored, 16 * NB)
            load_x1(NB - 1)

            def store_result(b, par):
                sp.wait_ge(res_ready, b + 1)
                sp.dma_start(out[bass.ds(b * BW, BW), :].rearrange("(t p) d -> p t d", p=P),
                             res[:, par, :, :]).then_inc(res_stored[par], 16)
            over_pairs(sp, store_result)
            for k in range(2):
                sp.wait_ge(res_stored[k], 16 * (NB // 2))

        @block.gpsimd
        def _(pool):
            nc.gpsimd.memset(ident[:, :], 0.0).then_inc(pool_step, 1)
            nc.gpsimd.memset(ones[:, :], 1.0).then_inc(consts_ready, 1)
            nc.gpsimd.iota(row_in_block[:, :], pattern=[[1, BW]], base=0, channel_multiplier=0).then_inc(consts_ready, 1)
            nc.gpsimd.iota(first_row[:, :], pattern=[[BW, NB]], base=0, channel_multiplier=0).then_inc(consts_ready, 1)
            pool.wait_ge(pool_step, 1)
            nc.gpsimd.affine_select(out=ident[:, :], in_=ident[:, :], compare_op=ALU.not_equal, fill=1.0, base=0,
                                    pattern=[[-1, P]], channel_multiplier=1).then_inc(consts_ready, 1)
            pool.dma_start(col0[:, :], adj[:, 0:1].rearrange("(p t) a -> p (t a)", p=P)).then_inc(col0_loaded, 16)

            for L in range(2):
                pool.wait_ge(feat_ready, (L + 1) * GROUPS)
                if L:
                    pool.wait_ge(epi_step[0], NB * EPI)
                for grp in range(1, GROUPS):
                    wait(pool, feat_totalled, L * (GROUPS - 1) + grp - 1)
                    before = feat[:, 0:4, :] if grp == 1 else feat_total
                    nc.gpsimd.tensor_tensor(feat_total, before, feat[:, 4 * grp:4 * grp + 4, :], ALU.add)\
                        .then_inc(feat_totalled, 1)

            def add_self_loops(b):
                pool.wait_ge(prob_ready[1], (b + 1) * UNITS)
                wait(pool, self_loops, b)
                diags = [adjT[:, b, b * RT + t, t * P:(t + 1) * P] for t in range(RT)]
                for t in range(RT):
                    last = nc.gpsimd.tensor_copy(diag_plus[:, t, :], diags[t])
                last.then_inc(diag_step, 1)
                pool.wait_ge(diag_step, 2 * b + 1)
                nc.gpsimd.tensor_tensor(diag_plus[:, :, :], diag_plus[:, :, :],
                                        ident_bf[:, :].rearrange("p (a i) -> p a i", a=1).broadcast_to([P, RT, P]),
                                        ALU.add).then_inc(diag_step, 1)
                pool.wait_ge(diag_step, 2 * b + 2)
                for t in range(RT):
                    last = nc.gpsimd.tensor_copy(diags[t], diag_plus[:, t, :])
                last.then_inc(self_loops, 1)

            def plain():
                for b in range(NB):
                    add_self_loops(b)

            def guarded():
                for b in range(NB):
                    wait(pool, shifted, b * UNITS)
                    wait(pool, epi_step[1], b * EPI)
                    pool.wait_ge(row_max_step, (b + 1) * UNITS * 2)
                    nc.gpsimd.partition_all_reduce(max_all[:, :], row_max[:, :], P, bass.bass_isa.ReduceOp.max)\
                        .then_inc(max_spread, 1)
                    add_self_loops(b)
            pool.wait_ge(ident_ready, 1)
            pool.wait_ge(chunk_summed, NB * UNITS)
            second_attention(pool, plain, guarded)
            for b in range(NB):
                rows = x1[:, RT * b:RT * (b + 1), :]
                pool.wait_ge(z_made, b + 1)
                nc.gpsimd.tensor_tensor(rows, rows, bg_all[:, :].rearrange("p (a d) -> p a d", a=1).broadcast_to([P, RT, P]),
                                        ALU.add).then_inc(x1_biased, 1)

        @block.scalar
        def _(act):
            x_rows = x.rearrange("(t p) d -> p t d", p=P)
            for part_x in range(LN):
                tiles = slice(LT * part_x, LT * (part_x + 1))
                act.dma_start(x_in[:, tiles, :], x_rows[:, tiles, :]).then_inc(x_loaded[part_x], 16)
            for k, w in enumerate((W0, W1, Wg)):
                act.dma_start(w_in[:, k, :], w).then_inc(w_loaded, 16)
            for k, b in enumerate((b0, b1)):
                act.dma_start(bias_col[:, k:k + 1], b.rearrange("(d a) -> d a", a=1)).then_inc(bias_loaded, 16)
            act.dma_start(bg_all[:, :], bg.rearrange("(a d) -> a d", a=1).broadcast_to([P, P])).then_inc(bias_loaded, 16)

            def keep_unit(b, u):
                act.wait_ge(chunk_turned, b * UNITS + u + 1)
                nc.scalar.activation(kept_place(b, u), turned, ACT.Copy).then_inc(kept_by_act, 1)

            def sum_unit(b, u):
                act.wait_ge(chunk_loaded[u % PAIRS], 16 * (b * (UNITS // PAIRS) + u // PAIRS + 1))
                wait(act, chunk_summed, b * UNITS + u)
                for c in range(2):
                    last = nc.scalar.activation(junk[:, c, :], chunk[:, u % PAIRS, c, :], ACT.Copy,
                                                accum_out=deg_part[:, bass.ds(b * CHUNKS + 2 * u + c, 1)])
                last.then_inc(chunk_summed, 1)

            def feat_copy(L, grp):
                act.wait_ge(feat_made, L * GROUPS + grp + 1)
                nc.scalar.activation(feat[:, 4 * grp:4 * grp + 4, :],
                                     feat_bank(L, grp).rearrange("p (t d) -> p t d", t=4),
                                     ACT.Copy).then_inc(feat_ready, 1)

            def x_root(part_x):
                act.wait_ge(var_ready, part_x + 1)
                tiles = slice(LT * part_x, LT * (part_x + 1))
                nc.scalar.activation(std[:, tiles], var_eps[:, tiles], ACT.Sqrt).then_inc(std_ready, 1)

            def high_of_x(grp):
                act.wait_ge(hT_turned, grp + 1)
                nc.scalar.activation(high[:, grp * BW:(grp + 1) * BW], group_bank(grp), ACT.Relu).then_inc(high_ready, 1)

            sum_unit(0, 0)
            keep_unit(0, 0)
            x_root(0)
            act.wait_ge(w_turned, 3)
            for k in range(2):
                nc.scalar.activation(WT_high[:, k, :], pMisc[:, k * P:(k + 1) * P], ACT.Copy).then_inc(w_high_ready, 1)
            nc.scalar.activation(WgT[:, :], pMisc[:, 3 * P:4 * P], ACT.Copy).then_inc(w_high_ready, 1)
            x_root(1)
            sum_unit(0, 1)
            keep_unit(0, 1)
            high_of_x(0)
            high_of_x(1)
            x_root(2)
            high_of_x(2)
            high_of_x(3)
            x_root(3)
            feat_copy(0, 0)
            feat_copy(0, 1)
            high_of_x(4)
            high_of_x(5)
            feat_copy(0, 2)
            feat_copy(0, 3)
            high_of_x(6)
            high_of_x(7)
            sum_unit(0, 2)
            keep_unit(0, 2)
            for grp in range(4, GROUPS):
                feat_copy(0, grp)
            sum_unit(0, 3)

            def epi_own(L, b):
                act.wait_ge(own_made[L], b + 1)
                wait(act, epi_step[L], b * EPI)
                nc.scalar.activation(tB[:, :], pMisc[:, :], ACT.Copy).then_inc(own_kept[L], 1)

            def epi_relu(L, b):
                act.wait_ge(epi_step[L], b * EPI + EPI)
                nc.scalar.activation(tC[:, :], tA[:, :], ACT.Relu, bias=bias_col[:, L:L + 1]).then_inc(relu_done[L], 1)
                if L == 0:
                    act.wait_ge(relu_done[L], b + 1)
                    if not (is_int(b) and b == NB - 1):
                        act.dma_start(h1T_dram[:, bass.ds(b * BW, BW)], tC[:, :]).then_inc(stored, 16)
                    nc.scalar.activation(tA[:, :], tC[:, :], ACT.Square).then_inc(square_ready, 1)

            def attention(L):
                def body(b, par, has_prev, has_next):
                    for u in range(UNITS):
                        g = b * UNITS + u
                        act.wait_ge(scores_ready[L], g + 1)
                        if not (is_int(b) and b == 0 and u < 2):
                            wait(act, prob_used[L], g - 1)
                            wait(act, prob_added[L], g - 1)
                        nc.scalar.activation(prob[:, u % 2, :, :], pS[:, u % 2, :, :], ACT.Exp,
                                             scale=SCALE).then_inc(exp_ready[L], 1)
                        ahead = turned_unit(b, u, has_next)
                        if L == 0 and ahead:
                            if not kept_by_vector(ahead[1]):
                                keep_unit(*ahead)
                            sum_unit(*ahead)
                        if has_prev and u == 1:
                            epi_own(L, b - 1)
                        if has_prev and u == 11:
                            epi_relu(L, b - 1)
                        if not has_next and u == UNITS - 1:
                            epi_own(L, b)
                over_blocks(act, body)

            act.wait_ge(bias_loaded, 48)
            attention(0)

            def high_of_h1(grp):
                if grp < GROUPS - 1:
                    act.wait_ge(h1_loaded[grp % 4], 16 * (grp // 4 + 1))
                    src = chunk[:, (grp // 2) % 2, grp % 2, :]
                else:
                    act.wait_ge(relu_done[0], NB)
                    src = tC[:, :]
                nc.scalar.activation(high[:, grp * BW:(grp + 1) * BW], src, ACT.Copy).then_inc(high_ready, 1)

            act.wait_ge(own_made[0], NB)
            act.wait_ge(scores_ready[0], NB * UNITS)
            high_of_h1(0)
            high_of_h1(1)
            act.wait_ge(prob_used[0], NB * UNITS)
            feat_copy(1, 0)
            for grp in range(2, 5):
                high_of_h1(grp)
                feat_copy(1, grp - 1)
            epi_relu(0, NB - 1)
            for grp in range(5, GROUPS):
                high_of_h1(grp)
                feat_copy(1, grp - 1)
            feat_copy(1, GROUPS - 1)

            def guarded():
                def body(b, has_next):
                    for u in range(UNITS):
                        act.wait_ge(shifted, b * UNITS + u + 1)
                        nc.scalar.activation(prob[:, u % 2, :, :], prob[:, u % 2, :, :], ACT.Exp,
                                             scale=SCALE).then_inc(exp_ready[1], 1)
                    epi_own(1, b)
                    if has_next:
                        epi_relu(1, b)
                one_by_one(act, body)
            second_attention(act, lambda: attention(1), guarded)

            def roots(batch):
                lo, hi = BATCH[batch]
                act.wait_ge(var2_ready, batch + 1)
                if batch == 0:
                    act.wait_ge(deg_ready, 1)
                    nc.scalar.activation(droot, deg, ACT.Sqrt)
                nc.scalar.activation(std2[:, lo:hi], var_eps2[:, lo:hi], ACT.Sqrt).then_inc(std2_ready, 1)

            def rows_and_high(grp):
                act.wait_ge(x1_loaded[grp], 16)
                act.wait_ge(scale_ready, 1 if grp < NB - 1 else 2)
                if grp >= 2:
                    act.wait_ge(z_low_ready, grp - 1)
                for t in range(RT):
                    col = RT * grp + t
                    last = nc.scalar.activation(z[:, grp % 2, t, :], x1[:, col, :], ACT.Relu,
                                                bias=row_shift[:, col:col + 1], scale=row_scale[:, col:col + 1])
                last.then_inc(z_made, 1)
                act.wait_ge(z_made, grp + 1)
                tiles = slice(RT * grp, RT * (grp + 1))
                nc.scalar.activation(z_high[:, tiles, :], z[:, grp % 2, :, :], ACT.Copy)\
                    .then_inc(z_high_ready, 1)

            def widen(b, t):
                if t < 2:
                    act.wait_ge(self_loops, b + 1)
                act.wait_ge(adj_used, b * NJ + t - SLOTS + 1)
                nc.scalar.activation(adj_wide[:, t % SLOTS, :], adj_tile(b, t), ACT.Copy).then_inc(wide_by_act, 1)

            def keep_agg(b, par):
                act.wait_ge(adj_used, (b + 1) * NJ)
                wait(act, res_made, b)
                nc.scalar.activation(aggT[:, :], pAcc[:, par, :], ACT.Copy).then_inc(agg_kept, 1)

            roots(0)
            act.wait_ge(own_made[1], NB)
            act.wait_ge(scores_ready[1], NB * UNITS)
            rows_and_high(0)
            rows_and_high(1)
            epi_relu(1, NB - 1)

            def body(b, par):
                if is_int(b) and b == 0:
                    for grp in range(2, GROUPS):
                        rows_and_high(grp)
                        if grp == 3:
                            roots(1)
                    return
                for t in range(NJ):
                    if widened_by_act(b, t):
                        widen(b, t)
                    if t == 1:
                        keep_agg(b - 1, 1 - par)
            over_pairs(act, body)
            keep_agg(NB - 1, 1)

        @block.vector
        def _(dve):
            def keep_unit(b, u):
                dve.wait_ge(chunk_turned, b * UNITS + u + 1)
                nc.vector.tensor_copy(kept_place(b, u), turned).then_inc(kept_by_dve, 1)

            dve.wait_ge(consts_ready, 4)
            nc.vector.tensor_copy(ident_bf[:, :], ident[:, :]).then_inc(ident_ready, 1)
            def x_variances(part_x):
                tiles = range(LT * part_x, LT * (part_x + 1))
                dve.wait_ge(x_loaded[part_x], 16)
                for t in tiles:
                    last = nc.vector.bn_stats(stats[:, t, :], x_in[:, t, :])
                last.then_inc(x_stats, 1)
                dve.wait_ge(x_stats, part_x + 1)
                for t in tiles:
                    last = nc.vector.bn_aggr(mean_var[:, t, :], stats[:, t, :])
                last.then_inc(x_means, 1)
                dve.wait_ge(x_means, part_x + 1)
                sl = slice(tiles[0], tiles[-1] + 1)
                nc.vector.tensor_scalar(var_eps[:, sl], mean_var[:, sl, 1], EPS_LN, None, ALU.add).then_inc(var_ready, 1)

            def x_normal(part_x):
                tiles = range(LT * part_x, LT * (part_x + 1))
                sl = slice(tiles[0], tiles[-1] + 1)
                dve.wait_ge(std_ready, part_x + 1)
                nc.vector.reciprocal(rstd[:, sl], std[:, sl]).then_inc(rstd_ready, 1)
                dve.wait_ge(rstd_ready, part_x + 1)
                for t in tiles:
                    last = nc.vector.tensor_scalar(h_in[:, t, :], x_in[:, t, :], mean_var[:, t, 0:1], rstd[:, t:t + 1],
                                                   ALU.subtract, ALU.mult)
                last.then_inc(h_ready, 1)

            def low_of_x(grp):
                cols = slice(grp * BW, (grp + 1) * BW)
                dve.wait_ge(high_ready, grp + 1)
                nc.vector.scalar_tensor_tensor(out=low[:, cols], in0=group_bank(grp), scalar=0.0,
                                               in1=high[:, cols].bitcast(F32), op0=ALU.max,
                                               op1=ALU.subtract).then_inc(low_ready, 1)

            x_variances(0)
            x_variances(1)
            x_normal(0)
            for k in range(2):
                dve.wait_ge(w_high_ready, 3)
                nc.vector.tensor_tensor(WT_low[:, k, :], pMisc[:, k * P:(k + 1) * P],
                                        WT_high[:, k, :].bitcast(F32), ALU.subtract).then_inc(w_low_ready, 1)
            x_normal(1)
            x_variances(2)
            low_of_x(0)
            low_of_x(1)
            x_normal(2)
            x_variances(3)
            low_of_x(2)
            low_of_x(3)
            x_normal(3)
            for grp in range(4, GROUPS):
                low_of_x(grp)
            dve.wait_ge(col0_loaded, 16)
            nc.vector.tensor_scalar(col0_set[:, :], col0[:, :], 0.0, None, ALU.not_equal).then_inc(col0_step, 1)
            dve.wait_ge(col0_step, 1)
            nc.vector.tensor_reduce(col0_sum[:, :], col0_set[:, :], AX_X, ALU.add).then_inc(col0_counted, 1)
            dve.wait_ge(consts_ready, 4)
            nc.vector.tensor_copy(first_row_f[:, :], first_row[:, :]).then_inc(col0_step, 1)
            dve.wait_ge(col0_step, 2)
            dve.wait_ge(col0_total, 1)
            nc.vector.tensor_scalar(left_in_block[:, :], first_row_f[:, :], -1.0, pMisc[:, 2 * P:2 * P + 1],
                                    ALU.mult, ALU.add).then_inc(rows_ready, 1)
            dve.wait_ge(rows_ready, 1)
            keep_unit(0, 3)

            def epilogue(L, b, par, step):
                s = epi_step[L]
                if step < INV:
                    if step == 0:
                        dve.wait_ge(den_made[L], b + 1)
                        if L == 0:
                            wait(dve, stored, b * 16)
                            wait(dve, square_ready, b)
                        else:
                            wait(dve, turned_back, b)
                    cols = slice(step * BW // INV, (step + 1) * BW // INV)
                    nc.vector.reciprocal(tC[:, cols], pMisc[:, cols]).then_inc(s, 1)
                elif step == INV:
                    dve.wait_ge(s, b * EPI + INV)
                    dve.wait_ge(prob_used[L], b * UNITS + UNITS)
                    if is_int(b) and b == 0:
                        dve.wait_ge(tiny_ready, L + 1)
                    nc.vector.scalar_tensor_tensor(out=tA[:, :], in0=pAcc[:, par, :], scalar=tiny_sum[:, L:L + 1],
                                                   in1=tC[:, :], op0=ALU.add, op1=ALU.mult).then_inc(s, 1)
                elif step == INV + 1:
                    dve.wait_ge(s, b * EPI + INV + 1)
                    dve.wait_ge(own_kept[L], b + 1)
                    nc.vector.tensor_tensor(tA[:, :], tA[:, :], tB[:, :], ALU.subtract).then_inc(s, 1)
                elif step == INV + 2:
                    dve.wait_ge(s, b * EPI + INV + 2)
                    left = left_in_block[:, b:b + 1] if is_int(b) else left_in_block[:, bass.ds(b, 1)]
                    nc.vector.scalar_tensor_tensor(out=tA[:, :], in0=row_in_block[:, :], scalar=left, in1=tA[:, :],
                                                   op0=ALU.is_ge, op1=ALU.mult).then_inc(s, 1)
                elif step == INV + 3:
                    dve.wait_ge(s, b * EPI + INV + 3)
                    nc.vector.scalar_tensor_tensor(out=tA[:, :], in0=tA[:, :], scalar=0.5, in1=tB[:, :],
                                                   op0=ALU.mult, op1=ALU.add).then_inc(s, 1)

            def steps_at(L, u):
                if L == 1:
                    return range(u - 3, u - 2) if 3 <= u < 3 + EPI else ()
                return {4: (0,), 5: (1,), 6: (2, 3), 8: (4, 5), 9: (6,), 10: (7,)}.get(u, ())

            def epi_norm(b):
                dve.wait_ge(norm_made, b + 1)
                dst = norm_max[:, b:b + 1] if is_int(b) else norm_max[:, bass.ds(b, 1)]
                nc.vector.tensor_reduce(dst, pMisc[:, :], AX_X, ALU.max).then_inc(norm_read, 1)

            def tiny(L):
                dve.wait_ge(feat_summed, L + 1)
                nc.vector.tensor_scalar(tiny_sum[:, L:L + 1], pMisc[:, 0:1], TINY, None, ALU.mult).then_inc(tiny_ready, 1)

            def residual(b):
                dve.wait_ge(turned_back, b + 1)
                dve.wait_ge(x_block_loaded, 16 * (b + 1))
                nc.vector.tensor_tensor(x_block[:, :, :], x_block[:, :, :],
                                        pMisc[:, :].rearrange("p (t d) -> p t d", t=RT), ALU.add).then_inc(x1_made, 1)

            def statistics(b):
                dve.wait_ge(x1_made, b + 1)
                for t in range(RT):
                    last = nc.vector.bn_stats(stats2[:, t, :], x_block[:, t, :])
                last.then_inc(stats_made, 1)
                dve.wait_ge(stats_made, b + 1)
                nc.vector.tensor_copy(stats_all[:, bass.ds(b * RT, RT), :], stats2[:, :, :]).then_inc(stats_kept, 1)

            def means(blocks):
                dve.wait_ge(stats_kept, blocks[-1] + 1)
                for b in blocks:
                    for t in range(RT * b, RT * (b + 1)):
                        last = nc.vector.bn_aggr(mean_var2[:, t, :], stats_all[:, t, :])
                    last.then_inc(mean_var_kept, 1)

            def attention(L):
                def body(b, par, has_prev, has_next):
                    for u in range(UNITS):
                        if L == 0 and u % 2 == 0:
                            by_act, by_dve = kept_before(b, u + 2)
                            dve.wait_ge(kept_by_act, by_act)
                            wait(dve, kept_by_dve, by_dve)
                        g = b * UNITS + u
                        pr = prob[:, u % 2, :, :]
                        a = adj_unit(b, u)
                        dve.wait_ge(exp_ready[L], g + 1)
                        nc.vector.tensor_tensor(pr, pr, a, ALU.mult).then_inc(prob_ready[L], 1)
                        ahead = turned_unit(b, u, has_next)
                        if L == 0 and ahead and kept_by_vector(ahead[1]):
                            keep_unit(*ahead)
                        add_unit(L, b, u)
                        if not has_prev and u == 10:
                            tiny(L)
                        if has_prev:
                            for step in steps_at(L, u):
                                epilogue(L, b - 1, 1 - par, step)
                        if has_prev and u == 14 and L == 0:
                            epi_norm(b - 1)
                        if has_prev and u == 13 and L == 1:
                            residual(b - 1)
                        if has_prev and u == 14 and L == 1:
                            statistics(b - 1)
                        if L == 1 and not has_next and u in (2, 3):
                            means(range(3 * u - 6, 3 * u - 3))
                        if L == 1 and not has_next and u == 15:
                            means(range(NB - 2, NB - 1))
                    keep_sum(L, b)

                over_blocks(dve, body)

            def add_unit(L, b, u):
                g = b * UNITS + u
                pr = prob[:, u % 2, :, :]
                dve.wait_ge(prob_ready[L], g + 1)
                if u == 0:
                    wait(dve, sum_kept[L], b)
                    nc.vector.tensor_scalar(psumR[:, :], pr[:, 0, :], (N // P) * TINY, None,
                                            ALU.add).then_inc(half_added[L], 1)
                else:
                    dve.wait_ge(prob_added[L], g)
                    nc.vector.tensor_tensor(psumR[:, :], psumR[:, :], pr[:, 0, :], ALU.add).then_inc(half_added[L], 1)
                dve.wait_ge(half_added[L], g + 1)
                nc.vector.tensor_tensor(psumR[:, :], psumR[:, :], pr[:, 1, :], ALU.add).then_inc(prob_added[L], 1)

            def keep_sum(L, b):
                dve.wait_ge(prob_added[L], b * UNITS + UNITS)
                if L == 0:
                    wait(dve, norm_made, b)
                else:
                    wait(dve, relu_done[L], b)
                nc.vector.tensor_copy(tA[:, :], psumR[:, :]).then_inc(sum_kept[L], 1)

            def guarded():
                def body(b, has_next):
                    if is_int(b) and b == 0:
                        tiny(1)
                    else:
                        dve.wait_ge(relu_done[1], b)
                        dve.wait_ge(prob_used[1], b * UNITS)
                    for u in range(UNITS):
                        g = b * UNITS + u
                        dve.wait_ge(scan_scores, g + 1)
                        wait(dve, row_max_step, 2 * g)
                        nc.vector.tensor_tensor(scan[:, :, :], pS[:, u % 2, :, :], adj_unit(b, u),
                                                ALU.mult).then_inc(masked, 1)
                        dve.wait_ge(masked, g + 1)
                        if u == 0:
                            wait(dve, max_spread, b)
                            nc.vector.tensor_copy(row_max[:, :], scan[:, 0, :]).then_inc(row_max_step, 1)
                        else:
                            nc.vector.tensor_tensor(row_max[:, :], row_max[:, :], scan[:, 0, :],
                                                    ALU.max).then_inc(row_max_step, 1)
                        dve.wait_ge(row_max_step, 2 * g + 1)
                        nc.vector.tensor_tensor(row_max[:, :], row_max[:, :], scan[:, 1, :],
                                                ALU.max).then_inc(row_max_step, 1)
                        dve.wait_ge(row_max_step, 2 * g + 2)
                    dve.wait_ge(max_spread, b + 1)
                    for u in range(UNITS):
                        g = b * UNITS + u
                        pr = prob[:, u % 2, :, :]
                        dve.wait_ge(scores_ready[1], g + 1)
                        if not (is_int(b) and b == 0 and u < 2):
                            dve.wait_ge(prob_used[1], g - 1)
                            dve.wait_ge(prob_added[1], g - 1)
                        for h in range(2):
                            last = nc.vector.tensor_tensor(pr[:, h, :], pS[:, u % 2, h, :], max_all[:, :],
                                                           ALU.subtract)
                        last.then_inc(shifted, 1)
                        dve.wait_ge(exp_ready[1], g + 1)
                        nc.vector.scalar_tensor_tensor(out=pr, in0=pr, scalar=3e38, in1=adj_unit(b, u),
                                                       op0=ALU.min, op1=ALU.mult).then_inc(prob_ready[1], 1)
                        add_unit(1, b, u)
                    keep_sum(1, b)
                    if has_next:
                        for step in range(EPI):
                            epilogue(1, b, 1, step)
                        residual(b)
                        statistics(b)
                    else:
                        means(range(NB - 1))
                one_by_one(dve, body)

            attention(0)

            def low_of_h1(grp):
                cols = slice(grp * BW, (grp + 1) * BW)
                src = chunk[:, (grp // 2) % 2, grp % 2, :] if grp < GROUPS - 1 else tC[:, :]
                dve.wait_ge(high_ready, GROUPS + grp + 1)
                nc.vector.tensor_tensor(low[:, cols], src, high[:, cols].bitcast(F32), ALU.subtract).then_inc(low_ready, 1)

            low_of_h1(0)
            low_of_h1(1)
            for step in range(EPI):
                epilogue(0, NB - 1, 1, step)
                if step in (1, 3, 5):
                    low_of_h1(2 + step // 2)
            low_of_h1(5)
            epi_norm(NB - 1)
            dve.wait_ge(norm_read, NB)
            nc.vector.tensor_reduce(largest[:, :], norm_max[:, :], AX_X, ALU.max).then_inc(largest_known, 1)
            dve.wait_ge(largest_known, 1)
            nc.vector.tensor_scalar(all_safe[:, :], largest[:, :], SAFE_SCORE / SCALE, None,
                                    ALU.is_le).then_inc(range_known, 1)
            for grp in range(6, GROUPS):
                low_of_h1(grp)
            nc.vector.tensor_reduce(deg.rearrange("p (b t) -> p b t", t=RT),
                                    deg_part[:, :].rearrange("p (b q t) -> p b t q", q=CPR, t=RT), AX_X,
                                    ALU.add).then_inc(deg_step, 1)
            dve.wait_ge(deg_step, 1)
            nc.vector.tensor_scalar(deg, deg, 1.0, None, ALU.add).then_inc(deg_ready, 1)
            second_attention(dve, lambda: attention(1), guarded)

            def variances(batch):
                lo, hi = BATCH[batch]
                dve.wait_ge(mean_var_kept, hi // RT)
                nc.vector.tensor_scalar(var_eps2[:, lo:hi], mean_var2[:, lo:hi, 1], EPS_LN, None,
                                        ALU.add).then_inc(var2_ready, 1)

            def scales(batch):
                lo, hi = BATCH[batch]
                dve.wait_ge(std2_ready, batch + 1)
                if batch == 0:
                    nc.vector.reciprocal(dinv, droot).then_inc(deg_step, 1)
                nc.vector.reciprocal(var_eps2[:, lo:hi], std2[:, lo:hi]).then_inc(scale_step, 1)
                dve.wait_ge(deg_step, 2)
                dve.wait_ge(scale_step, 2 * batch + 1)
                nc.vector.tensor_tensor(row_scale[:, lo:hi], var_eps2[:, lo:hi], dinv[:, lo:hi],
                                        ALU.mult).then_inc(scale_step, 1)
                dve.wait_ge(scale_step, 2 * batch + 2)
                nc.vector.scalar_tensor_tensor(out=row_shift[:, lo:hi], in0=mean_var2[:, lo:hi, 0], scalar=-1.0,
                                               in1=row_scale[:, lo:hi], op0=ALU.mult,
                                               op1=ALU.mult).then_inc(scale_ready, 1)

            def low_of_z(grp):
                dve.wait_ge(z_high_ready, grp + 1)
                tiles = slice(RT * grp, RT * (grp + 1))
                nc.vector.tensor_tensor(z_low[:, tiles, :], z[:, grp % 2, :, :],
                                        z_high[:, tiles, :].bitcast(F32), ALU.subtract).then_inc(z_low_ready, 1)

            def widen(b, t):
                if t < 2:
                    dve.wait_ge(self_loops, b + 1)
                if not (is_int(b) and b == 0 and t < SLOTS):
                    dve.wait_ge(adj_used, b * NJ + t - SLOTS + 1)
                nc.vector.tensor_copy(adj_wide[:, t % SLOTS, :], adj_tile(b, t)).then_inc(wide_by_dve, 1)

            variances(0)
            scales(0)
            dve.wait_ge(prob_used[1], NB * UNITS)
            for t in range(SLOTS):
                widen(0, t)
            for step in range(EPI):
                epilogue(1, NB - 1, 1, step)
                if step in (1, INV + 1):
                    low_of_z((step - 1) // INV)

            def body(b, par):
                first = is_int(b) and b == 0
                for t in range(NJ):
                    if first and t % 4 == 0 and t >= 8:
                        low_of_z(t // 4)
                    if not widened_by_act(b, t) and not (first and t < SLOTS):
                        widen(b, t)
                    if first and t == 6:
                        residual(NB - 1)
                        statistics(NB - 1)
                        means(range(NB - 1, NB))
                        variances(1)
                    if first and t == 15:
                        scales(1)
                    if t == FINISH and not first:
                        finish(b - 1, 1 - par)

            def finish(b, par):
                dve.wait_ge(res_made, b + 1)
                dve.wait_ge(x1_biased, NB)
                if not (is_int(b) and b < 2):
                    dve.wait_ge(res_stored[par], (b - par) * 8)
                for t in range(RT):
                    row = b * RT + t
                    last = nc.vector.scalar_tensor_tensor(
                        out=res[:, par, t, :], in0=pMisc[:, t * P:(t + 1) * P], scalar=scal2[:, 2, bass.ds(row, 1)],
                        in1=x1[:, bass.ds(row, 1), :].rearrange("p a d -> p (a d)"), op0=ALU.mult, op1=ALU.add)
                last.then_inc(res_ready, 1)
            over_pairs(dve, body)
            finish(NB - 1, 1)

        @block.tensor
        def _(pe):
            pe.wait_ge(consts_ready, 4)

            def turn_unit(b, u):
                pe.wait_ge(chunk_loaded[u % PAIRS], 16 * (b * (UNITS // PAIRS) + u // PAIRS + 1))
                by_act, by_dve = kept_before(b, u)
                if u % 4:
                    pe.wait_ge(kept_by_act, by_act)
                else:
                    wait(pe, kept_by_dve, by_dve)
                for c in range(2):
                    upper = chunk[:, u % PAIRS, c, :].bitcast(BF16).rearrange("p (j two) -> p j two", two=2)[:, :, 1]
                    for m in range(4):
                        mm = nc.tensor.transpose(pT[:, m, c, :], upper[:, m * P:(m + 1) * P], ident_bf[:, :])
                mm.then_inc(chunk_turned, 1)

            def product3(dst, a_high, a_low, b_high, b_low):
                nc.tensor.matmul(dst, a_high, b_high, start=True, stop=False)
                nc.tensor.matmul(dst, a_high, b_low, start=False, stop=False)
                return nc.tensor.matmul(dst, a_low, b_high, start=False, stop=True)

            def make_feat(L, grp):
                pe.wait_ge(low_ready, L * GROUPS + grp + 1)
                ring = 2 if L == 0 else 4
                if grp >= ring:
                    pe.wait_ge(feat_ready, L * GROUPS + grp - ring + 1)
                for t in range(4 * grp, 4 * grp + 4):
                    mm = product3(feat_bank(L, grp)[:, (t % 4) * P:(t % 4 + 1) * P],
                                  high[:, t * P:(t + 1) * P], low[:, t * P:(t + 1) * P],
                                  WT_high[:, L, :], WT_low[:, L, :])
                mm.then_inc(feat_made, 1)

            def sum_feat(L):
                if L == 0:
                    pe.wait_ge(rows_ready, 1)
                pe.wait_ge(feat_totalled, (L + 1) * (GROUPS - 1))
                for t in range(4):
                    mm = nc.tensor.matmul(pMisc[:, 0:1], feat_total[:, t, :], ones[:, 0:1], start=(t == 0), stop=(t == 3))
                mm.then_inc(feat_summed, 1)

            def turn_h(grp):
                pe.wait_ge(h_ready, grp // 2 + 1)
                if grp >= 4:
                    pe.wait_ge(low_ready, grp - 3)
                for t in range(4 * grp, 4 * grp + 4):
                    mm = nc.tensor.transpose(group_bank(grp)[:, (t % 4) * P:(t % 4 + 1) * P], h_in[:, t, :], ident[:, :])
                mm.then_inc(hT_turned, 1)

            pe.wait_ge(ident_ready, 1)
            turn_unit(0, 0)
            turn_unit(0, 1)
            pe.wait_ge(w_loaded, 48)
            for k, at_col in enumerate((0, P, 3 * P)):
                nc.tensor.transpose(pMisc[:, at_col:at_col + P], w_in[:, k, :], ident[:, :]).then_inc(w_turned, 1)
            for grp in range(4):
                turn_h(grp)
            pe.wait_ge(w_low_ready, 2)
            make_feat(0, 0)
            make_feat(0, 1)
            turn_h(4)
            turn_h(5)
            make_feat(0, 2)
            make_feat(0, 3)
            turn_h(6)
            turn_h(7)
            turn_unit(0, 2)
            for grp in range(4, GROUPS):
                make_feat(0, grp)
            turn_unit(0, 3)
            pe.wait_ge(col0_counted, 1)
            nc.tensor.matmul(pMisc[:, 2 * P:2 * P + 1], ones[:, :], col0_sum[:, :], start=True, stop=True)\
                .then_inc(col0_total, 1)
            pe.wait_ge(feat_ready, GROUPS)

            def unit_scores(b, u):
                rows = bass.ds(b * BW, BW)
                for h in range(2):
                    t = 2 * u + h
                    mm = product3(pS[:, u % 2, h, :], high[:, t * P:(t + 1) * P], low[:, t * P:(t + 1) * P],
                                  high[:, rows], low[:, rows])
                return mm

            def scores(L, b, u):
                if not (is_int(b) and b == 0 and u < 2):
                    pe.wait_ge(exp_ready[L], b * UNITS + u - 1)
                unit_scores(b, u).then_inc(scores_ready[L], 1)

            def own(L, b):
                if L == 0:
                    wait(pe, norm_read, b)
                else:
                    wait(pe, x1_made, b)
                if is_int(b) and b == 0:
                    pe.wait_ge(tiny_ready, L + 1)
                rows = bass.ds(b * BW, BW)
                product3(pMisc[:, :], WT_high[:, L, :], WT_low[:, L, :], high[:, rows], low[:, rows])\
                    .then_inc(own_made[L], 1)

            def denominator(L, b):
                pe.wait_ge(own_kept[L], b + 1)
                pe.wait_ge(sum_kept[L], b + 1)
                nc.tensor.matmul(pMisc[:, :], ones[:, :], tA[:, :], start=True, stop=True).then_inc(den_made[L], 1)

            def norms(b):
                pe.wait_ge(square_ready, b + 1)
                nc.tensor.matmul(pMisc[:, :], ones[:, :], tA[:, :], start=True, stop=True).then_inc(norm_made, 1)

            def turn_back(b):
                pe.wait_ge(relu_done[1], b + 1)
                for t in range(RT):
                    mm = nc.tensor.transpose(pMisc[:, t * P:(t + 1) * P], tC[:, t * P:(t + 1) * P], ident[:, :])
                mm.then_inc(turned_back, 1)

            def mix(L, b, par, u):
                pe.wait_ge(prob_ready[L], b * UNITS + u + 1)
                for h in range(2):
                    mm = nc.tensor.matmul(pAcc[:, par, :], feat[:, 2 * u + h, :], prob[:, u % 2, h, :],
                                          start=(u == 0 and h == 0), stop=(u == UNITS - 1 and h == 1))
                mm.then_inc(prob_used[L], 1)

            def attention(L):
                def body(b, par, has_prev, has_next):
                    for u in range(UNITS):
                        ahead = turned_unit(b, u, has_next)
                        if L == 0 and ahead:
                            turn_unit(*ahead)
                        if L == 1 and not has_prev and u == 0:
                            pe.wait_ge(feat_ready, 2 * GROUPS)
                        if u < UNITS - 1:
                            scores(L, b, u + 1)
                        elif has_next:
                            scores(L, b + 1, 0)
                        if not has_prev and u == 8:
                            sum_feat(L)
                        if has_prev and u == 1:
                            own(L, b - 1)
                        if has_prev and u == 2:
                            denominator(L, b - 1)
                        if has_prev and u == 12:
                            norms(b - 1) if L == 0 else turn_back(b - 1)
                        if not has_next and u == 14:
                            own(L, b)
                        if u == 0 and not (is_int(b) and b < 2):
                            pe.wait_ge(epi_step[L], (b - 1) * EPI)
                        mix(L, b, par, u)

                scores(L, 0, 0)
                over_blocks(pe, body)

            def guarded():
                def body(b, has_next):
                    if is_int(b) and b == 0:
                        pe.wait_ge(feat_ready, 2 * GROUPS)
                        sum_feat(1)
                    for u in range(UNITS):
                        g = b * UNITS + u
                        if u < 2:
                            wait(pe, shifted, b * UNITS)
                        else:
                            pe.wait_ge(row_max_step, 2 * g - 2)
                        unit_scores(b, u).then_inc(scan_scores, 1)
                    pe.wait_ge(max_spread, b + 1)
                    for u in range(UNITS):
                        if u >= 2:
                            pe.wait_ge(shifted, b * UNITS + u - 1)
                        unit_scores(b, u).then_inc(scores_ready[1], 1)
                        if u >= 1:
                            if u == 1:
                                wait(pe, epi_step[1], b * EPI)
                            mix(1, b, 1, u - 1)
                    mix(1, b, 1, UNITS - 1)
                    own(1, b)
                    if has_next:
                        denominator(1, b)
                        turn_back(b)
                one_by_one(pe, body)

            attention(0)
            denominator(0, NB - 1)
            pe.wait_ge(exp_ready[0], NB * UNITS)
            for grp in range(5):
                make_feat(1, grp)
            norms(NB - 1)
            for grp in range(5, GROUPS):
                make_feat(1, grp)
            pe.wait_ge(norm_read, NB)
            pe.wait_ge(feat_ready, 2 * GROUPS - 2)
            second_attention(pe, lambda: attention(1), guarded)

            denominator(1, NB - 1)

            def body(b, par):
                for t in range(NJ):
                    by_act, by_dve = widened_before(b, t)
                    if widened_by_act(b, t):
                        pe.wait_ge(wide_by_act, by_act + 1)
                    else:
                        pe.wait_ge(wide_by_dve, by_dve + 1)
                    if is_int(b) and b == 0 and t % 4 == 0:
                        pe.wait_ge(z_low_ready, t // 4 + 1)
                    if t == 0 and not (is_int(b) and b < 2):
                        pe.wait_ge(agg_kept, b - 1)
                    nc.tensor.matmul(pAcc[:, par, :], z_high[:, t, :], adj_wide[:, t % SLOTS, :], start=(t == 0), stop=False)
                    nc.tensor.matmul(pAcc[:, par, :], z_low[:, t, :], adj_wide[:, t % SLOTS, :], start=False,
                                     stop=(t == NJ - 1)).then_inc(adj_used, 1)
                    if is_int(b) and b == 0 and t == 3:
                        turn_back(NB - 1)
                    if t == PROJECT and not (is_int(b) and b == 0):
                        project(b - 1)

            def project(b):
                pe.wait_ge(agg_kept, b + 1)
                wait(pe, res_ready, b)
                pe.wait_ge(x1_made, NB)
                for t in range(RT):
                    mm = nc.tensor.matmul(pMisc[:, t * P:(t + 1) * P], aggT[:, t * P:(t + 1) * P], WgT[:, :],
                                          start=True, stop=True)
                mm.then_inc(res_made, 1)
            over_pairs(pe, body)
            project(NB - 1)


_INS = ['x', 'adj', 'L0_gnn_W0', 'L0_gnn_b0', 'L0_gnn_W1', 'L0_gnn_b1', 'L1_gnn_W', 'L1_gnn_b']
_OUTS = [((4096, 128), 'float32')]


def kernel(**inputs):
    import numpy as _np
    import concourse.bacc as _bacc
    from concourse import mybir as _mybir
    from concourse.bass_utils import run_bass_kernel_spmd as _run

    nc = _bacc.Bacc("TRN2", target_bir_lowering=False, num_devices=1)
    arrays, args = {}, []
    for name in _INS:
        a = _np.ascontiguousarray(inputs[name])
        arrays[f"in_{name}_dram"] = a
        args.append(nc.dram_tensor(f"in_{name}_dram", a.shape, _mybir.dt.from_np(a.dtype), kind="ExternalInput").ap())
    for i, (shape, dtype) in enumerate(_OUTS):
        dt = _mybir.dt.from_np(_np.dtype(dtype))
        args.append(nc.dram_tensor(f"out_{i}_dram", shape, dt, kind="ExternalOutput").ap())
    build(nc, *args)
    r = _run(nc, [arrays], core_ids=[0])
    return r.results[0]["out_0_dram"]
```
